# Optimizing a Trainium2 kernel written in Bass

```python
import numpy as np
import jax
import jax.numpy as jnp

def _softmax(x, axis=-1):
    return jax.nn.softmax(x, axis=axis)

def _gelu(x):
    return jax.nn.gelu(x, approximate=True)

def _silu(x):
    return jax.nn.silu(x)

def _sigmoid(x):
    return jax.nn.sigmoid(x)

def _layernorm(x, axis=-1, eps=1e-05):
    m = jnp.mean(x, axis=axis, keepdims=True)
    v = jnp.var(x, axis=axis, keepdims=True)
    return (x - m) / jnp.sqrt(v + eps)

def _scatter_add(tgt, idx, src, axis=0):
    return tgt.at[idx].add(src)

def _segment_sum(src, seg, n):
    return jax.ops.segment_sum(src, seg, n)
kernel_name = 'mk_adj_ffn_d1_adj_r2_63d396'

def setup_inputs(seed: int=0):
    np.random.seed(seed)
    _w = jnp.asarray

    def _rec_inputs():
        import jax
        import jax.numpy as jnp
        _gk = jax.random.key(seed)
        x = -0.0005146 + 1 * jax.random.normal(jax.random.fold_in(_gk, 1), (8, 1024, 128), jnp.float32)
        _w = (1.0 + jnp.arange(1024, dtype=jnp.float32)) ** (-0.5)
        _w = _w / _w.mean()
        _pij = jnp.clip(0.0078125 * _w[:, None] * _w[None, :], 0.0, 1.0)
        _a = jax.random.uniform(jax.random.fold_in(_gk, 2), (8, 1024, 1024)) < _pij
        adj = _a.astype(jnp.int32)
        return (x, adj)
    x, adj = _rec_inputs()

    def _L0_gnn_setup():
        import jax, jax.numpy as jnp
        import numpy as np
        B, N, C, OUT, S = (4, 1024, 128, 128, 25)
        DENSITY = 0.008
        key = jax.random.key(seed)
        kA, kX, kW = jax.random.split(key, 3)
        A = jax.random.bernoulli(kA, DENSITY, (B, N, N)).astype(jnp.int32)
        X = jax.random.normal(kX, (B, N, C), dtype=jnp.float32)
        W = jax.random.normal(kW, (2 * C, OUT), dtype=jnp.float32) * np.float32(1.0 / np.sqrt(2 * C))
        b = jnp.zeros((OUT,), dtype=jnp.float32)
        return {'A': A, 'X': X, 'W': W, 'b': b}
    _L0_gnn_all = _L0_gnn_setup()
    _L0_gnn_in = {k: v for k, v in _L0_gnn_all.items() if k in ('W', 'b')}
    del _L0_gnn_all

    def _L0_ffn_setup():
        import jax, jax.numpy as jnp
        import numpy as np
        B, T, IN_DIM = (64, 128, 128)
        HID, OUT_DIM = (256, 128)
        N_LAYERS, N_EXPERTS, N_SHARED = (2, 16, 1)
        key = jax.random.key(seed)
        ks = jax.random.split(key, 10)
        s = 0.02
        x = jax.random.normal(ks[0], (B, T, IN_DIM), dtype=jnp.float32)
        route_id = jax.random.randint(ks[1], (B,), 0, N_EXPERTS)
        Wi = jax.random.normal(ks[2], (HID, IN_DIM), dtype=jnp.float32) * s
        bi = jnp.zeros((HID,), dtype=jnp.float32)
        Wr = jax.random.normal(ks[3], (N_LAYERS, N_EXPERTS, HID, HID), dtype=jnp.float32) * s
        br = jax.random.normal(ks[4], (N_LAYERS, N_EXPERTS, HID), dtype=jnp.float32) * s
        Ws = jax.random.normal(ks[5], (N_LAYERS, N_SHARED, HID, HID), dtype=jnp.float32) * s
        bs = jax.random.normal(ks[6], (N_LAYERS, N_SHARED, HID), dtype=jnp.float32) * s
        Wo = jax.random.normal(ks[7], (OUT_DIM, HID), dtype=jnp.float32) * s
        bo = jnp.zeros((OUT_DIM,), dtype=jnp.float32)
        return {'x': x, 'route_id': route_id, 'Wi': Wi, 'bi': bi, 'Wr': Wr, 'br': br, 'Ws': Ws, 'bs': bs, 'Wo': Wo, 'bo': bo}
    _L0_ffn_all = _L0_ffn_setup()
    _L0_ffn_in = {k: v for k, v in _L0_ffn_all.items() if k in ('route_id', 'Wi', 'bi', 'Wr', 'br', 'Ws', 'bs', 'Wo', 'bo')}
    del _L0_ffn_all
    return {'x': x, 'adj': adj, 'L0_gnn_W': _L0_gnn_in['W'], 'L0_gnn_b': _L0_gnn_in['b'], 'L0_ffn_route_id': _L0_ffn_in['route_id'], 'L0_ffn_Wi': _L0_ffn_in['Wi'], 'L0_ffn_bi': _L0_ffn_in['bi'], 'L0_ffn_Wr': _L0_ffn_in['Wr'], 'L0_ffn_br': _L0_ffn_in['br'], 'L0_ffn_Ws': _L0_ffn_in['Ws'], 'L0_ffn_bs': _L0_ffn_in['bs'], 'L0_ffn_Wo': _L0_ffn_in['Wo'], 'L0_ffn_bo': _L0_ffn_in['bo']}

def reference(x, adj, L0_gnn_W, L0_gnn_b, L0_ffn_route_id, L0_ffn_Wi, L0_ffn_bi, L0_ffn_Wr, L0_ffn_br, L0_ffn_Ws, L0_ffn_bs, L0_ffn_Wo, L0_ffn_bo):
    import jax
    import jax.numpy as jnp

    def _L0_gnn_ref(A, X, W, b):
        import jax, jax.numpy as jnp
        import numpy as np
        B, N, C, OUT, S = (4, 1024, 128, 128, 25)
        DENSITY = 0.008
        mask = A != 0
        neg_inf = jnp.float32(-jnp.inf)
        pri = -jnp.arange(N, dtype=jnp.float32)
        scores = jnp.where(mask, pri, neg_inf)
        vals, idx = jax.lax.top_k(scores, S)
        valid = vals > neg_inf
        feats = jax.vmap(lambda x, i: x[i])(X, idx)
        feats = jnp.where(valid[..., None], feats, neg_inf)
        agg = feats.max(axis=2)
        degree = mask.sum(axis=-1)
        agg = jnp.where((degree <= S)[..., None], jnp.maximum(agg, 0.0), agg)
        h = jnp.concatenate([X, agg], axis=-1)
        out = jax.nn.relu(jnp.einsum('bnf,fo->bno', h, W) + b)
        return out

    def _L0_ffn_ref(x, route_id, Wi, bi, Wr, br, Ws, bs, Wo, bo):
        import jax, jax.numpy as jnp
        import numpy as np
        B, T, IN_DIM = (64, 128, 128)
        HID, OUT_DIM = (256, 128)
        N_LAYERS, N_EXPERTS, N_SHARED = (2, 16, 1)
        flat = x.reshape(-1, x.shape[-1])
        n_tok = flat.shape[0]
        route = jnp.repeat(route_id, n_tok // route_id.shape[0])
        h = jax.nn.relu(flat @ Wi.T + bi)
        n_layers, n_experts = (Wr.shape[0], Wr.shape[1])
        for l in range(n_layers):
            shared = (jnp.einsum('nd,shd->snh', h, Ws[l]) + bs[l][:, None, :]).mean(axis=0)
            routed = jnp.zeros_like(h)
            for e in range(n_experts):
                ye = h @ Wr[l, e].T + br[l, e]
                routed = routed + jnp.where((route == e)[:, None], ye, 0.0)
            h = jax.nn.relu(shared + routed + h)
        out = h @ Wo.T + bo
        return out.reshape(*x.shape[:-1], out.shape[-1])
    x = x + _L0_gnn_ref(adj, _layernorm(x, axis=-1), L0_gnn_W, L0_gnn_b)
    x = x + _L0_ffn_ref(_layernorm(x, axis=-1), L0_ffn_route_id, L0_ffn_Wi, L0_ffn_bi, L0_ffn_Wr, L0_ffn_br, L0_ffn_Ws, L0_ffn_bs, L0_ffn_Wo, L0_ffn_bo)
    return x

_drawn_inputs = setup_inputs


def setup_inputs(seed=0):
    import zlib

    import numpy as np

    out = dict(_drawn_inputs(seed))
    spreads = {'L0_gnn_b': (0.0, 0.1), 'L0_ffn_bi': (0.0, 0.409), 'L0_ffn_bo': (0.0, 0.1)}
    factors = {'L0_ffn_Wr': 2.997, 'L0_ffn_br': 8.0, 'L0_ffn_Ws': 3.058, 'L0_ffn_bs': 8.0}
    for name, (base, spread) in spreads.items():
        noise = np.random.default_rng([zlib.crc32(name.encode()), seed]).standard_normal(out[name].shape)
        drawn = base * np.exp(spread * noise) if base else spread * noise
        out[name] = jnp.asarray(drawn.astype(out[name].dtype))
    for name, factor in factors.items():
        out[name] = (out[name] * factor).astype(out[name].dtype)
    return out
```

```python
from contextlib import ExitStack

import concourse.bass as bass
from concourse import mybir

F32 = mybir.dt.float32
BF16 = mybir.dt.bfloat16
I32 = mybir.dt.int32
ALU = mybir.AluOpType
ACT = mybir.ActivationFunctionType
AX_X = mybir.AxisListType.X

P = 128
TOPK = 25
ROUNDS = 4
EPS = 1e-5
NEG_BIG = -3.0e38
HUBS = 2
CHUNKS = 2
POS = 10
GROUPS = [(0, 1), (1, 1), (2, 2), (4, 2), (6, 2)]
SPLITS = 3


def gnn_ffn_program(nc, x, adj, gnn_W, gnn_b, route_id, Wi, bi, Wr, br, Ws, bs, Wo, bo, out):
    B, N, C = x.shape
    IT = N // P
    T = B * IT
    TT = IT - HUBS
    CW = TT * P // CHUNKS
    HID = Wi.shape[0]
    HC = HID // P
    L, NE = Wr.shape[0], Wr.shape[1]
    E1 = NE + 1
    NB = L * NE + L + 1
    NG = len(GROUPS)
    TABROW = N + 1
    WROW = HC * HID + HC
    NW = L * E1
    ZROWS = 16
    ZEROS = B * N // (P * ZROWS) + 1
    CONSTS = NG + 8
    RANK_AT = {7: [0, 1, 2], 8: [3, 4, 5], 9: [6, 7]}
    assert POS == CHUNKS * NG and HC == 2 and L == 2

    x_t = x.rearrange("b (t p) c -> b p t c", p=P)
    adj_t = adj.rearrange("b (t p) n -> (b t) p n", p=P)
    out_t = out.rearrange("b (t p) c -> b p t c", p=P)
    out_rows = out.rearrange("b (t p) c -> (b t) p c", p=P)
    table = nc.dram_tensor("feature_table", [B * TABROW, C], F32, kind="Internal").ap()
    table_b = table.rearrange("(b r) c -> b r c", b=B)
    folded = nc.dram_tensor("folded_weights", [L * E1, P, WROW], F32, kind="Internal").ap()
    wr_t = Wr.rearrange("l e (j p) d -> (l e) p j d", p=P)
    ws_t = Ws.rearrange("l s (j p) d -> (l s) p j d", p=P)

    with ExitStack() as ctx:
        def sb(name, shape, dt=F32):
            return ctx.enter_context(nc.sbuf_tensor(name, shape, dt))

        def pb(name, shape, dt=F32):
            return ctx.enter_context(nc.psum_tensor(name, shape, dt))

        def sem(name):
            return ctx.enter_context(nc.semaphore(name))

        ident = sb("ident", [P, P])
        identb = sb("identb", [P, P], BF16)
        before = sb("before", [P, P], BF16)
        onesb = sb("onesb", [P, P], BF16)
        pick = sb("pick", [P, IT, NG + 1], BF16)
        ones_row = sb("ones_row", [1, P])
        down = sb("down", [P, N])
        ranks = sb("ranks", [P, 32])
        base = sb("base", [P, B])
        gw = sb("gw", [P, 2, C])
        gb = sb("gb", [1, C])
        bo_row = sb("bo_row", [1, C])
        wiT = sb("wiT", [P, HID])
        woT = sb("woT", [P, HC, C])
        wsI = sb("wsI", [P, L, HC * HID])
        biasT = sb("biasT", [P, HC, NB])
        bias = sb("bias", [P, E1, L, HC])
        route_f = sb("route_f", [1, 2, T])
        route = sb("route", [1, T], I32)
        route_in = sb("route_in", [1, T], I32)

        xs = sb("xs", [P, T, C])
        mean1 = sb("mean1", [P, T])
        rstd1 = sb("rstd1", [P, T])
        shift1 = sb("shift1", [P, T])
        stats = sb("stats", [P, IT, 6])
        mv = sb("mv", [P, IT, 2])
        std = sb("std", [P, IT])
        newton = sb("newton", [P, 2, IT])
        xn = sb("xn", [P, IT, C])
        rest = sb("rest", [P, IT, C])
        xsplit = sb("xsplit", [P, 2, SPLITS, IT, C], BF16)

        adj_sb = sb("adj_sb", [P, 4, N], I32)
        mask = sb("mask", [P, 2, N], BF16)
        at = sb("at", [P, IT, TT * P], BF16)
        rank = sb("rank", [P, 2, IT, TT * P], BF16)
        onehot = sb("onehot", [P, 2, 2, CW], BF16)
        acc = sb("acc", [P, 2, CW])
        aggT = sb("aggT", [P, TT * P])
        most = sb("most", [NG + 1, B * TT])
        most_any = sb("most_any", [NG + 1, 1])
        over = sb("over", [NG + 1, B * TT], I32)
        over_any = sb("over_any", [NG + 1, 1], I32)
        mostc = sb("mostc", [NG + 1, 2, CHUNKS])
        pairs = sb("pairs", [NG + 1, 2, CHUNKS], I32)

        score = sb("score", [P, HUBS, N])
        top = sb("top", [P, HUBS, 8 * ROUNDS])
        idx = sb("idx", [P, HUBS, TOPK], I32)
        floor = sb("floor", [P, HUBS])
        gath = sb("gath", [P, TOPK, C])
        hub_max = sb("hub_max", [P, C])
        hub = sb("hub", [P, HUBS, C])
        hubT = sb("hubT", [P, HUBS, C])

        xnf = sb("xnf", [P, IT, C])
        xnT = sb("xnT", [P, IT, C])
        x1 = sb("x1", [P, IT, C])
        st2 = sb("st2", [P, IT, 6])
        mv2 = sb("mv2", [P, IT, 2])
        std2 = sb("std2", [P, IT])
        r2 = sb("r2", [P, IT])
        h0 = sb("h0", [P, IT, C])
        h0T = xnT
        hT = sb("hT", [P, 2, HC, IT, P])
        wst = sb("wst", [P, IT, WROW])
        y = h0
        w_in = xnf[:, :, :].rearrange("p t c -> p (t c)").rearrange("p (a j d) -> p a j d", a=2, j=HC)
        wi_in = xnT[:, 0:HC, :]
        wo_in = xnT[:, HC:2 * HC, :].rearrange("p a c -> p (a c)")
        bias_in = xnT[0:NB, 2 * HC:3 * HC, :].rearrange("p a c -> p (a c)")
        NIN = 2
        NST = 4

        slot_ps = [pb(f"slot_ps{i}", [P, 512]) for i in range(2)]
        prep_ps = [pb(f"prep_ps{i}", [P, 1024], BF16) for i in range(2)]
        ffn_ps = [pb(f"ffn_ps{i}", [P, 512]) for i in range(4)]
        prep_f = [p[:, :].bitcast(F32) for p in prep_ps]

        s_memset = sem("s_memset")
        s_const = sem("s_const")
        s_zero = sem("s_zero")
        s_x = [sem(f"s_x{b}") for b in range(4)]
        s_small = sem("s_small")
        s_wload = [sem(f"s_wload{i}") for i in range(NIN)]
        s_wT = sem("s_wT")
        s_wfold = sem("s_wfold")
        s_wstore = [sem(f"s_wstore{i}") for i in range(NST)]
        s_route = sem("s_route")
        s_var1 = sem("s_var1")
        s_std1 = sem("s_std1")
        s_xn = sem("s_xn")
        s_hi = sem("s_hi")
        s_rest = sem("s_rest")
        s_mid = sem("s_mid")
        s_split = sem("s_split")
        s_tab = [sem(f"s_tab{i}") for i in range(2)]
        s_adj = [sem(f"s_adj{i}") for i in range(4)]
        s_scored = sem("s_scored")
        s_mask = sem("s_mask")
        s_tr = sem("s_tr")
        s_at = sem("s_at")
        s_cnt = sem("s_cnt")
        s_pairs = sem("s_pairs")
        s_rank = sem("s_rank")
        s_q = sem("s_q")
        s_onehot = sem("s_onehot")
        s_slot = sem("s_slot")
        s_max = sem("s_max")
        s_agg = sem("s_agg")
        s_idx = sem("s_idx")
        s_gath = sem("s_gath")
        s_hubred = sem("s_hubred")
        s_hub = sem("s_hub")
        s_xnf = sem("s_xnf")
        s_nT = sem("s_nT")
        s_nTc = sem("s_nTc")
        s_gnn = sem("s_gnn")
        s_var2 = sem("s_var2")
        s_std2 = sem("s_std2")
        s_h0 = sem("s_h0")
        s_h0T = sem("s_h0T")
        s_h0c = sem("s_h0c")
        s_in = sem("s_in")
        s_inr = sem("s_inr")
        s_l = [sem(f"s_l{l}") for l in range(L)]
        s_r = [sem(f"s_r{l}") for l in range(L)]
        s_w = [sem(f"s_w{i}") for i in range(IT)]
        s_o = sem("s_o")
        s_y = sem("s_y")
        s_out = [sem(f"s_out{i}") for i in range(2)]

        s_over = sem("s_over")
        r_adj = sem("r_adj")
        r_w = [sem(f"r_w{l}") for l in range(L)]
        r_idx = sem("r_idx")
        r_gath = sem("r_gath")
        r_hub = sem("r_hub")
        r_xn = sem("r_xn")
        r_T = sem("r_T")
        r_Tc = sem("r_Tc")
        r_gnn = sem("r_gnn")
        r_var = sem("r_var")
        r_std = sem("r_std")
        r_h0 = sem("r_h0")
        r_h0T = sem("r_h0T")
        r_h0c = sem("r_h0c")
        r_in = sem("r_in")
        r_inr = sem("r_inr")
        r_l = [sem(f"r_l{l}") for l in range(L)]
        r_r = [sem(f"r_r{l}") for l in range(L)]
        r_o = sem("r_o")
        r_y = sem("r_y")
        r_stored = sem("r_stored")

        block = ctx.enter_context(nc.Block())

        def rounds(eng, body):
            body(0, 0, True, False, False)
            body(1, 1, True, True, False)
            body(2, 0, True, True, True)
            body(3, 1, True, True, True)
            with eng.Fori(2, B // 2) as q:
                body(q * 2, 0, True, True, True)
                body(q * 2 + 1, 1, True, True, True)
            body(B, 0, False, True, True)
            body(B + 1, 1, False, False, True)

        def again(eng, body):
            one = eng.alloc_register(f"again_{eng.engine.name}")
            dma = eng.alloc_register(f"again16_{eng.engine.name}")
            eng.reg_mov(one, 0)
            eng.reg_mov(dma, 0)
            eng.wait_ge(s_over, 1)
            some_over = eng.value_load(over_any[NG:NG + 1, 0:1], min_val=0, max_val=1)
            with eng.If(some_over > 0):
                with eng.Fori(0, B) as b:
                    with eng.Fori(0, TT) as i:
                        is_over = eng.value_load(over[NG:NG + 1, bass.ds(b * TT + i, 1)], min_val=0, max_val=1)
                        with eng.If(is_over > 0):
                            eng.reg_add(one, one, 1)
                            eng.reg_add(dma, dma, 16)
                            body(b * IT + HUBS + i, b, one, dma)

        def some(t, n=1):
            return slice(t, t + n) if isinstance(t, int) else bass.ds(t, n)

        def weights_of(s, n):
            if not isinstance(s, int) or s > 1:
                return []
            return [m for m in range(2 * (POS * s + n), 2 * (POS * s + n) + 2) if m < NW]

        def matrix(m):
            return (m, NE) if m < L else ((m - L) // NE, (m - L) % NE)

        @block.sync
        def _(sp):
            def load_x(first, many, signal):
                for b in range(first, first + many):
                    sp.dma_start(xs[:, b * IT:(b + 1) * IT, :], x_t[b]).then_inc(s_x[signal], 16)

            load_x(0, 1, 0)
            for a in range(4):
                sp.dma_start(adj_sb[:, a, :], adj_t[(a + HUBS) % IT]).then_inc(s_adj[a], 16)
            sp.dma_start(wi_in, Wi.rearrange("(j p) d -> p j d", p=P)).then_inc(s_small, 16)
            sp.dma_start(wo_in, Wo).then_inc(s_small, 16)
            sp.dma_start(bias_in[0:L * NE], br.rearrange("l e h -> (l e) h")).then_inc(s_small, 16)
            sp.dma_start(bias_in[L * NE:L * NE + L], bs.rearrange("l s h -> (l s) h")).then_inc(s_small, 16)
            sp.dma_start(bias_in[NB - 1:NB], bi.rearrange("(a n) -> a n", a=1)).then_inc(s_small, 16)
            sp.dma_start(gw[:, :, :], gnn_W.rearrange("(j p) d -> p j d", p=P)).then_inc(s_small, 16)
            sp.dma_start(gb[:, :], gnn_b.rearrange("(a n) -> a n", a=1)).then_inc(s_small, 16)
            sp.dma_start(bo_row[:, :], bo.rearrange("(a n) -> a n", a=1)).then_inc(s_small, 16)
            sp.dma_start(route_in[:, :], route_id.rearrange("(a n) -> a n", a=1)).then_inc(s_small, 16)
            for m in range(NIN):
                sp.dma_start(w_in[:, m], ws_t[m]).then_inc(s_wload[m], 16)
            load_x(1, 1, 1)
            load_x(2, 2, 2)
            load_x(4, B - 4, 3)

            def round_(s, even, prep, slots, ffn):
                k = s - 2
                for n in range(POS):
                    if ffn and n == 0:
                        for i in range(IT):
                            e = sp.value_load(route[0:1, some(k * IT + i)], min_val=0, max_val=NE)
                            if i == 0 and not (isinstance(s, int) and s == 2):
                                sp.wait_ge(s_r[1], k * IT)
                            sp.dma_start(wst[:, i, :], folded[bass.ds(e, 1)].rearrange("a p w -> (a p) w")
                                         ).then_inc(s_w[i], 16)
                    if prep and n < IT and not (isinstance(s, int) and s == 0 and n < 4):
                        if n >= 4:
                            sp.wait_ge(s_mask, s * TT + n - 3)
                        elif n < 2:
                            sp.wait_ge(s_mask, s * TT + n - 1)
                        else:
                            sp.wait_ge(s_scored, s * HUBS + n - 3)
                        sp.dma_start(adj_sb[:, n % 4, :], adj_t[some(s * IT + (n + HUBS) % IT)].rearrange(
                            "a p n -> (a p) n") if not isinstance(s, int) else adj_t[s * IT + (n + HUBS) % IT]
                                     ).then_inc(s_adj[n % 4], 16)
                    if prep and n == 2:
                        if isinstance(s, int) and s == 0:
                            sp.wait_ge(s_zero, 16 * ZEROS)
                        sp.wait_ge(s_xn, s + 1)
                        sp.dma_start(table_b[some(s), 0:N, :].rearrange("a (t p) c -> (a p) t c", p=P), xn[:, :, :]
                                     ).then_inc(s_tab[even], 16)
                    for m in weights_of(s, n):
                        if m + NIN < NW:
                            sp.wait_ge(s_wT, m + 2)
                            sp.dma_start(w_in[:, m % NIN], ws_t[m + NIN] if m + NIN < L else wr_t[m + NIN - L]
                                         ).then_inc(s_wload[m % NIN], 16)
                    if ffn and n == 6:
                        for i in range(IT):
                            e = sp.value_load(route[0:1, some(k * IT + i)], min_val=0, max_val=NE)
                            sp.wait_ge(s_r[0], k * IT + i + 1)
                            sp.dma_start(wst[:, i, :], folded[bass.ds(e + E1, 1)].rearrange("a p w -> (a p) w")
                                         ).then_inc(s_w[i], 16)

            def all_rounds(s, even, prep, slots, ffn):
                round_(s, even, prep, slots, ffn)
                if isinstance(s, int) and s == 1:
                    sp.wait_ge(s_route, 1)
                    for i in range(NST):
                        sp.wait_ge(s_wstore[i], 16 * len(range(i, NW, NST)))
            rounds(sp, all_rounds)

            for g in range(2):
                sp.wait_ge(s_out[g], 16 * B)

            def tile_again(t, b, one, dma):
                sp.dma_start(adj_sb[:, 0, :], adj_t[bass.ds(t, 1)].rearrange("a p n -> (a p) n")).then_inc(r_adj, 16)
                e = sp.value_load(route[0:1, bass.ds(t, 1)], min_val=0, max_val=NE)
                for l in range(L):
                    sp.dma_start(wst[:, l, :], folded[bass.ds(e + l * E1, 1)].rearrange("a p w -> (a p) w")
                                 ).then_inc(r_w[l], 16)
                sp.wait_ge(s_const, CONSTS)
                sp.wait_ge(r_y, one)
                sp.dma_start(out_rows[bass.ds(t, 1)].rearrange("a p c -> (a p) c"), y[:, 0, :]).then_inc(r_stored, 16)
                sp.wait_ge(s_const, CONSTS)
                sp.wait_ge(r_stored, dma)
            again(sp, tile_again)

        @block.gpsimd
        def _(pool):
            pool.memset(ident[:, :], 0.0).then_inc(s_memset, 1)
            pool.memset(onesb[:, :], 1.0).then_inc(s_memset, 1)
            pool.memset(pick[:, :, :], 0.0).then_inc(s_memset, 1)
            pool.wait_ge(s_memset, 3)
            pool.affine_select(out=ident[:, :], in_=ident[:, :], compare_op=ALU.not_equal, fill=1.0,
                               base=0, pattern=[[-1, P]], channel_multiplier=1).then_inc(s_memset, 1)
            pool.affine_select(out=before[:, :], in_=onesb[:, :], compare_op=ALU.is_gt, fill=0.0,
                               base=0, pattern=[[1, P]], channel_multiplier=-1).then_inc(s_memset, 1)
            pool.wait_ge(s_memset, 5)
            pool.affine_select(out=before[:, :], in_=before[:, :], compare_op=ALU.not_equal, fill=256.0,
                               base=0, pattern=[[1, P]], channel_multiplier=-1).then_inc(s_const, 1)
            pool.tensor_copy(identb[:, :], ident[:, :]).then_inc(s_const, 1)
            for g, (first, many) in enumerate(GROUPS):
                pool.memset(pick[:, first:first + many, g:g + 1], 1.0).then_inc(s_const, 1)
            pool.memset(pick[:, :, NG:NG + 1], 1.0).then_inc(s_const, 1)
            pool.memset(ones_row[:, :], 1.0).then_inc(s_const, 1)
            pool.iota(down[:, :], [[-1, N]], N, channel_multiplier=0,
                      allow_small_or_imprecise_dtypes=True).then_inc(s_const, 1)
            pool.iota(ranks[:, :], [[1, 32]], 1, channel_multiplier=0,
                      allow_small_or_imprecise_dtypes=True).then_inc(s_const, 1)
            pool.iota(base[:, :], [[TABROW, B]], N, channel_multiplier=0,
                      allow_small_or_imprecise_dtypes=True).then_inc(s_const, 1)
            pool.memset(gath[:, 0:ZROWS, :], 0.0).then_inc(s_const, 1)
            pool.wait_ge(s_const, CONSTS)
            for z in range(0, B * N, P * ZROWS):
                pool.dma_start(table[z:z + P * ZROWS].rearrange("(p t) c -> p t c", p=P), gath[:, 0:ZROWS, :]
                               ).then_inc(s_zero, 16)
            pool.dma_start(table[B * N:B * TABROW], gath[0:B, 0, :]).then_inc(s_zero, 16)
            pool.wait_ge(s_zero, 16 * ZEROS)
            tiles_ready, tiles_used, stored = (pool.alloc_register(r) for r in ("tiles_ready", "tiles_used", "stored"))
            pool.reg_mov(tiles_ready, 0)
            pool.reg_mov(tiles_used, 0)
            pool.reg_mov(stored, 0)

            def graph(par, first):
                if par == 0:
                    pool.reg_add(stored, stored, 16)
                for h in range(HUBS):
                    skip = first and par == 0 and h == 0
                    pool.reg_add(tiles_ready, tiles_ready, 1)
                    if not skip:
                        pool.reg_add(tiles_used, tiles_used, 1)
                    pool.wait_ge(s_const, CONSTS)
                    pool.wait_ge(s_idx, tiles_ready)
                    pool.wait_ge(s_tab[par], stored)
                    if not skip:
                        pool.wait_ge(s_hubred, tiles_used)
                    for j in range(TOPK):
                        pool.indirect_dma_start(gath[:, j, :], None, table,
                                                bass.IndirectOffsetOnAxis(ap=idx[:, h, j:j + 1], axis=0)
                                                ).then_inc(s_gath, 16)
            graph(0, True)
            graph(1, True)
            with pool.Fori(1, B // 2):
                graph(0, False)
                graph(1, False)

            def tile_again(t, b, one, dma):
                pool.wait_ge(s_const, CONSTS)
                pool.wait_ge(r_idx, one)
                for j in range(TOPK):
                    pool.indirect_dma_start(gath[:, j, :], None, table,
                                            bass.IndirectOffsetOnAxis(ap=idx[:, 0, j:j + 1], axis=0)
                                            ).then_inc(r_gath, 16)
            again(pool, tile_again)

        @block.scalar
        def _(act):
            act.wait_ge(s_const, CONSTS)

            def round_(s, even, prep, slots, ffn):
                k = s - 2
                for n in range(POS):
                    for m in weights_of(s, n):
                        l, e = matrix(m)
                        act.wait_ge(s_wfold, m + 1)
                        act.dma_start(folded[l * E1 + e], wst[:, m % NST, :]).then_inc(s_wstore[m % NST], 16)
                    if prep:
                        if n == 0:
                            act.wait_ge(s_var1, s + 1)
                            act.activation(std[:, :], mv[:, :, 1], ACT.Sqrt).then_inc(s_std1, 1)
                        if n == 2:
                            act.wait_ge(s_xn, s + 1)
                            if ffn:
                                act.wait_ge(s_agg, CHUNKS * (s - 1))
                            act.activation(xsplit[:, even, 0], xn[:, :, :], ACT.Copy).then_inc(s_hi, 1)
                        if n == 4:
                            act.wait_ge(s_rest, s + 1)
                            act.activation(xsplit[:, even, 1], rest[:, :, :], ACT.Copy).then_inc(s_mid, 1)
                    if ffn:
                        if n == 0:
                            for g in range(3):
                                act.wait_ge(s_nT, 3 * k + g + 1)
                                if g < 2:
                                    act.activation(xnT[:, 4 * g:4 * g + 4, :].rearrange("p t c -> p (t c)"),
                                                   ffn_ps[g][:, :], ACT.Copy).then_inc(s_nTc, 1)
                                else:
                                    act.activation(hubT[:, :, :].rearrange("p t c -> p (t c)"),
                                                   ffn_ps[2][:, 0:HUBS * C], ACT.Copy).then_inc(s_nTc, 1)
                        if n == 2:
                            act.wait_ge(s_var2, k + 1)
                            act.activation(std2[:, :], mv2[:, :, 1], ACT.Sqrt).then_inc(s_std2, 1)
                        if n == 3:
                            for g in range(2):
                                act.wait_ge(s_h0T, 2 * k + g + 1)
                                act.activation(h0T[:, 4 * g:4 * g + 4, :].rearrange("p t c -> p (t c)"),
                                               ffn_ps[g][:, :], ACT.Copy).then_inc(s_h0c, 1)
                        if n == 4:
                            for g in range(2):
                                act.wait_ge(s_in, 2 * k + g + 1)
                                for j in range(HC):
                                    ins = act.activation(hT[:, 0, j, 4 * g:4 * g + 4, :].rearrange("p t c -> p (t c)"),
                                                         ffn_ps[2 * (1 - g) + j][:, :], ACT.Relu,
                                                         bias=biasT[:, j, NB - 1:NB])
                                ins.then_inc(s_inr, 1)
                        if n in (5, 7):
                            l = (n - 5) // 2
                            for i in range(IT):
                                act.wait_ge(s_l[l], k * IT + i + 1)
                                for j in range(HC):
                                    c0 = (i // 4) * HID + j * P
                                    ins = act.activation(hT[:, 1 - l, j, i, :], ffn_ps[i % 4][:, c0:c0 + P],
                                                         ACT.Relu, bias=wst[:, i, HC * HID + j:HC * HID + j + 1])
                                ins.then_inc(s_r[l], 1)
                    if prep:
                        if n < TT:
                            act.wait_ge(s_tr, s * TT + n + 1)
                            if n == 0 and not (isinstance(s, int) and s == 0):
                                act.wait_ge(s_rank, 2 * IT * s)
                            act.activation(at[:, :, n * P:(n + 1) * P],
                                           prep_ps[n % 2][:, :].rearrange("p (j i) -> p j i", j=IT),
                                           ACT.Copy).then_inc(s_at, 1)
                        for jt in RANK_AT.get(n, []):
                            for c in range(CHUNKS):
                                act.wait_ge(s_rank, 2 * IT * s + 2 * jt + c + 1)
                                if jt == 0 and c == 0 and ffn:
                                    act.wait_ge(s_agg, CHUNKS * (s - 1))
                                act.activation(rank[:, even, jt, c * CW:(c + 1) * CW], prep_f[c][:, 0:CW],
                                               ACT.Copy, bias=-255.0).then_inc(s_q, 1)
                    if ffn and n == POS - 1:
                        for g in range(2):
                            act.wait_ge(s_y, k * 2 + g + 1)
                            act.dma_start(out_t[some(k), :, 4 * g:4 * g + 4, :].rearrange("a p t c -> (a p) t c"),
                                          y[:, 4 * g:4 * g + 4, :]).then_inc(s_out[g], 16)
                    if slots and n == POS - 1:
                        if ffn:
                            act.wait_ge(s_nT, 3 * (s - 1))
                        elif isinstance(s, int):
                            act.wait_ge(s_wT, NW + 1)
                        for i in range(IT):
                            t = some((s - 1) * IT + i)
                            ins = act.activation(xnf[:, i, :], xs[:, t, :].rearrange("p a c -> p (a c)"),
                                                 ACT.Identity, bias=shift1[:, t], scale=rstd1[:, t])
                        ins.then_inc(s_xnf, 1)
            rounds(act, round_)

            def tile_again(t, b, one, dma):
                one_tile = bass.ds(t, 1)
                act.wait_ge(s_const, CONSTS)
                act.wait_ge(r_adj, dma)
                act.activation(xnf[:, 0, :], xs[:, one_tile, :].rearrange("p a c -> p (a c)"), ACT.Identity,
                               bias=shift1[:, one_tile], scale=rstd1[:, one_tile]).then_inc(r_xn, 1)
                act.wait_ge(s_const, CONSTS)
                act.wait_ge(r_T, one)
                act.activation(xnT[:, 0, :], ffn_ps[0][:, 0:C], ACT.Copy)
                act.activation(hubT[:, 0, :], ffn_ps[1][:, 0:C], ACT.Copy).then_inc(r_Tc, 1)
                act.wait_ge(s_const, CONSTS)
                act.wait_ge(r_var, one)
                act.activation(std2[:, 0:1], mv2[:, 0, 1:2], ACT.Sqrt).then_inc(r_std, 1)
                act.wait_ge(s_const, CONSTS)
                act.wait_ge(r_h0T, one)
                act.activation(h0T[:, 0, :], ffn_ps[1][:, 0:C], ACT.Copy).then_inc(r_h0c, 1)
                act.wait_ge(s_const, CONSTS)
                act.wait_ge(r_in, one)
                for j in range(HC):
                    ins = act.activation(hT[:, 0, j, 0, :], ffn_ps[2][:, j * P:(j + 1) * P], ACT.Relu,
                                         bias=biasT[:, j, NB - 1:NB])
                ins.then_inc(r_inr, 1)
                for l in range(L):
                    act.wait_ge(s_const, CONSTS)
                    act.wait_ge(r_l[l], one)
                    for j in range(HC):
                        ins = act.activation(hT[:, 1 - l, j, 0, :], ffn_ps[l][:, j * P:(j + 1) * P], ACT.Relu,
                                             bias=wst[:, l, HC * HID + j:HC * HID + j + 1])
                    ins.then_inc(r_r[l], 1)
            again(act, tile_again)

        @block.tensor
        def _(pe):
            pe.wait_ge(s_const, CONSTS)
            slots_done = pe.alloc_register("slots_done")
            pe.reg_mov(slots_done, 0)

            def slot(even, first, many, c, bank):
                pe.reg_add(slots_done, slots_done, 1)
                pe.wait_ge(s_onehot, slots_done)
                pe.wait_ge(s_max, slots_done)
                for j in range(many):
                    for p in range(SPLITS):
                        mm = pe.matmul(slot_ps[bank][:, 0:CW], xsplit[:, even, p, first + j, :],
                                       onehot[:, bank, j, :], start=(j == 0 and p == 0),
                                       stop=(j == many - 1 and p == SPLITS - 1))
                mm.then_inc(s_slot, 1)

            def round_(s, even, prep, slots, ffn):
                k = s - 2
                for n in range(POS):
                    if isinstance(s, int) and s == 0 and n == 0:
                        pe.wait_ge(s_small, 9 * 16)
                        for j in range(HC):
                            pe.transpose(ffn_ps[2][:, j * P:(j + 1) * P], wi_in[:, j, :], ident[:, :])
                        for j in range(HC):
                            pe.transpose(ffn_ps[2][:, (HC + j) * P:(HC + j + 1) * P], wo_in[:, j * P:(j + 1) * P],
                                         ident[:, :])
                        for j in range(HC):
                            mm = pe.transpose(ffn_ps[3][:, j * NB:(j + 1) * NB], bias_in[:, j * P:(j + 1) * P],
                                              ident[0:NB, 0:NB])
                        mm.then_inc(s_wT, 1)
                    for m in weights_of(s, n):
                        l, e = matrix(m)
                        pe.wait_ge(s_wload[m % NIN], 16 * (m // NIN + 1))
                        if m >= 2:
                            pe.wait_ge(s_wfold, m - 1)
                        for kc in range(HC):
                            for hc in range(HC):
                                mm = pe.transpose(ffn_ps[m % 2][:, (kc * HC + hc) * P:(kc * HC + hc + 1) * P],
                                                  w_in[:, m % NIN, hc, kc * P:(kc + 1) * P], ident[:, :])
                        mm.then_inc(s_wT, 1)
                    if ffn:
                        if n == 0:
                            pe.wait_ge(s_xnf, k + 1)
                            if isinstance(s, int) and s == 2:
                                pe.wait_ge(s_wfold, NW)
                            else:
                                pe.wait_ge(s_y, 2 * k)
                            for i in range(IT):
                                mm = pe.transpose(ffn_ps[i // 4][:, (i % 4) * P:(i % 4 + 1) * P], xnf[:, i, :],
                                                  ident[:, :])
                                if i % 4 == 3:
                                    mm.then_inc(s_nT, 1)
                            pe.wait_ge(s_hub, HUBS * (k + 1))
                            for h in range(HUBS):
                                mm = pe.transpose(ffn_ps[2][:, h * P:(h + 1) * P], hub[:, h, :], ident[:, :])
                            mm.then_inc(s_nT, 1)
                        if n == 1:
                            pe.wait_ge(s_nTc, 3 * k + 3)
                            pe.wait_ge(s_agg, CHUNKS * (k + 1))
                            for i in range(IT):
                                o = ffn_ps[i // 4][:, (i % 4) * P:(i % 4 + 1) * P]
                                a = hubT[:, i, :] if i < HUBS else aggT[:, (i - HUBS) * P:(i - HUBS + 1) * P]
                                pe.matmul(o, xnT[:, i, :], gw[:, 0, :], start=True, stop=False)
                                pe.matmul(o, a, gw[:, 1, :], start=False, stop=False)
                                mm = pe.matmul(o, ones_row[:, :], gb[:, :], start=False, stop=True)
                                if i % 4 == 3:
                                    mm.then_inc(s_gnn, 1)
                        if n == 3:
                            pe.wait_ge(s_h0, k + 1)
                            for i in range(IT):
                                mm = pe.transpose(ffn_ps[i // 4][:, (i % 4) * P:(i % 4 + 1) * P], h0[:, i, :],
                                                  ident[:, :])
                                if i % 4 == 3:
                                    mm.then_inc(s_h0T, 1)
                        if n == 4:
                            for g in range(2):
                                pe.wait_ge(s_h0c, 2 * k + 1 + g)
                                for j in range(HC):
                                    mm = pe.matmul(ffn_ps[2 * (1 - g) + j][:, :], wiT[:, j * P:(j + 1) * P],
                                                   h0T[:, 4 * g:4 * g + 4, :].rearrange("p t c -> p (t c)"),
                                                   start=True, stop=True)
                                mm.then_inc(s_in, 1)
                        if n in (5, 7):
                            l = (n - 5) // 2
                            if l == 0:
                                pe.wait_ge(s_inr, 2 * k + 2)
                            for i in range(IT):
                                pe.wait_ge(s_w[i], (k * L + l + 1) * 16)
                                if l == 1 and i == 0:
                                    pe.wait_ge(s_r[0], (k + 1) * IT)
                                if i >= 4:
                                    pe.wait_ge(s_r[l], k * IT + i - 3)
                                for j in range(HC):
                                    c1 = (i // 4) * HID + j * P
                                    for kc in range(HC):
                                        c0 = kc * HID + j * P
                                        mm = pe.matmul(ffn_ps[i % 4][:, c1:c1 + P], wst[:, i, c0:c0 + P],
                                                       hT[:, l, kc, i, :], start=(kc == 0), stop=(kc == HC - 1))
                                mm.then_inc(s_l[l], 1)
                        if n == 8:
                            pe.wait_ge(s_r[1], (k + 1) * IT)
                            for i in range(IT):
                                o = ffn_ps[i // 4][:, (i % 4) * P:(i % 4 + 1) * P]
                                for kc in range(HC):
                                    pe.matmul(o, hT[:, 0, kc, i, :], woT[:, kc, :], start=(kc == 0), stop=False)
                                mm = pe.matmul(o, ones_row[:, :], bo_row[:, :], start=False, stop=True)
                                if i % 4 == 3:
                                    mm.then_inc(s_o, 1)
                    if slots:
                        c, g = n // NG, n % NG
                        first, many = GROUPS[g]
                        if n == 0:
                            pe.wait_ge(s_const, CONSTS)
                            pe.wait_ge(s_pairs, s)
                            pe.wait_ge(s_split, s)
                        K = pe.value_load(pairs[g:g + 1, 1 - even, c:c + 1], min_val=2, max_val=(TOPK + 1) // 2)
                        with pe.Fori(0, K):
                            for bank in range(2):
                                slot(1 - even, first, many, c, bank)
                    if prep:
                        if n < TT:
                            pe.wait_ge(s_mask, s * TT + n + 1)
                            if n >= 2:
                                pe.wait_ge(s_at, s * TT + n - 1)
                            elif not (isinstance(s, int) and s == 0):
                                pe.wait_ge(s_q, 2 * IT * s)
                            for jt in range(IT):
                                mm = pe.transpose(prep_ps[n % 2][:, jt * P:(jt + 1) * P],
                                                  mask[:, n % 2, jt * P:(jt + 1) * P], identb[:, :])
                            mm.then_inc(s_tr, 1)
                        if n == TT:
                            pe.wait_ge(s_at, (s + 1) * TT)
                            for c in range(CHUNKS):
                                for jt in range(IT):
                                    mm = pe.matmul(prep_f[c][0:NG + 1, 0:CW], pick[:, jt, :],
                                                   at[:, jt, c * CW:(c + 1) * CW], start=(jt == 0),
                                                   stop=(jt == IT - 1))
                            mm.then_inc(s_cnt, 1)
                        for jt in RANK_AT.get(n, []):
                            second = [f for f, many in GROUPS if many == 2 and f + 1 == jt]
                            for c in range(CHUNKS):
                                if jt == 0:
                                    pe.wait_ge(s_pairs, s + 1)
                                else:
                                    pe.wait_ge(s_q, 2 * IT * s + 2 * jt + c - 1)
                                cols = slice(c * CW, (c + 1) * CW)
                                mm = pe.matmul(prep_f[c][:, 0:CW], before[:, :], at[:, jt, cols],
                                               start=True, stop=not second)
                                if second:
                                    mm = pe.matmul(prep_f[c][:, 0:CW], onesb[:, :], at[:, jt - 1, cols],
                                                   start=False, stop=True)
                                mm.then_inc(s_rank, 1)
            rounds(pe, round_)

            def tile_again(t, b, one, dma):
                pe.wait_ge(s_const, CONSTS)
                pe.wait_ge(r_xn, one)
                pe.transpose(ffn_ps[0][:, 0:P], xnf[:, 0, :], ident[:, :])
                pe.wait_ge(s_const, CONSTS)
                pe.wait_ge(r_hub, one)
                pe.transpose(ffn_ps[1][:, 0:P], hub[:, 0, :], ident[:, :]).then_inc(r_T, 1)
                pe.wait_ge(s_const, CONSTS)
                pe.wait_ge(r_Tc, one)
                pe.matmul(ffn_ps[0][:, 0:C], xnT[:, 0, :], gw[:, 0, :], start=True, stop=False)
                pe.matmul(ffn_ps[0][:, 0:C], hubT[:, 0, :], gw[:, 1, :], start=False, stop=False)
                pe.matmul(ffn_ps[0][:, 0:C], ones_row[:, :], gb[:, :], start=False, stop=True).then_inc(r_gnn, 1)
                pe.wait_ge(s_const, CONSTS)
                pe.wait_ge(r_h0, one)
                pe.transpose(ffn_ps[1][:, 0:P], h0[:, 0, :], ident[:, :]).then_inc(r_h0T, 1)
                pe.wait_ge(s_const, CONSTS)
                pe.wait_ge(r_h0c, one)
                for j in range(HC):
                    mm = pe.matmul(ffn_ps[2][:, j * P:(j + 1) * P], wiT[:, j * P:(j + 1) * P], h0T[:, 0, :],
                                   start=True, stop=True)
                mm.then_inc(r_in, 1)
                for l in range(L):
                    pe.wait_ge(s_const, CONSTS)
                    pe.wait_ge(r_w[l], dma)
                    pe.wait_ge(r_r[l - 1] if l else r_inr, one)
                    for j in range(HC):
                        for kc in range(HC):
                            c0 = kc * HID + j * P
                            mm = pe.matmul(ffn_ps[l][:, j * P:(j + 1) * P], wst[:, l, c0:c0 + P],
                                           hT[:, l, kc, 0, :], start=(kc == 0), stop=(kc == HC - 1))
                    mm.then_inc(r_l[l], 1)
                pe.wait_ge(s_const, CONSTS)
                pe.wait_ge(r_r[L - 1], one)
                for kc in range(HC):
                    pe.matmul(ffn_ps[3][:, 0:C], hT[:, 0, kc, 0, :], woT[:, kc, :], start=(kc == 0), stop=False)
                pe.matmul(ffn_ps[3][:, 0:C], ones_row[:, :], bo_row[:, :], start=False, stop=True).then_inc(r_o, 1)
            again(pe, tile_again)

        @block.vector
        def _(dve):
            def step(ins):
                dve.drain()

            slots_seen = dve.alloc_register("slots_seen")
            dve.reg_mov(slots_seen, 0)
            dve.wait_ge(s_const, CONSTS)
            dve.memset(acc[:, 0, 0:1], 0.0).then_inc(s_max, 1)
            dve.memset(acc[:, 1, 0:1], 0.0).then_inc(s_max, 1)

            def newton_rstd(out_r, v, sd, tmp):
                r, e = tmp[:, 0, :], tmp[:, 1, :]
                step(dve.reciprocal(r, sd))
                step(dve.tensor_tensor(e, r, r, ALU.mult))
                step(dve.tensor_tensor(e, e, v, ALU.mult))
                step(dve.tensor_scalar(e, e, -0.5, 1.5, ALU.mult, ALU.add))
                step(dve.tensor_tensor(out_r, r, e, ALU.mult))

            def one_hot(par, first, many, c, bank, r):
                dve.tensor_scalar(onehot[:, bank, 0:many, :], rank[:, par, first:first + many, c * CW:(c + 1) * CW],
                                  r, None, ALU.is_equal).then_inc(s_onehot, 1)

            def fold_slot(bank):
                dve.tensor_tensor(acc[:, bank, :], slot_ps[bank][:, 0:CW], acc[:, bank, :],
                                  ALU.max).then_inc(s_max, 1)

            def next_slot():
                dve.reg_add(slots_seen, slots_seen, 1)
                dve.wait_ge(s_slot, slots_seen)

            def round_(s, even, prep, slots, ffn):
                k = s - 2
                for n in range(POS):
                    if prep:
                        if n < TT:
                            dve.wait_ge(s_adj[n % 4], 32 * s + 16 * (n // 4 + 1))
                            if n >= 2 or not (isinstance(s, int) and s == 0):
                                dve.wait_ge(s_tr, s * TT + n - 1)
                            dve.tensor_scalar(mask[:, n % 2, :], adj_sb[:, n % 4, :], 0.0, None,
                                              ALU.not_equal).then_inc(s_mask, 1)
                    if prep:
                        prepare(s, even, n)
                    for m in weights_of(s, n):
                        fold_weights(m)
                    if slots:
                        c, g = n // NG, n % NG
                        first, many = GROUPS[g]
                        par = 1 - even
                        if g == 0:
                            dve.drain()
                        if n == 0:
                            dve.wait_ge(s_q, 2 * IT * s)
                            dve.wait_ge(s_pairs, s)
                        if g == 0:
                            dve.memset(acc[:, :, :], 0.0)
                        K = dve.value_load(pairs[g:g + 1, par, c:c + 1], min_val=2, max_val=(TOPK + 1) // 2)
                        for bank in range(2):
                            one_hot(par, first, many, c, bank, ranks[:, bank:bank + 1])
                        with dve.Fori(1, K) as j:
                            for bank in range(2):
                                next_slot()
                                one_hot(par, first, many, c, bank, ranks[:, bass.ds(j * 2 + bank, 1)])
                                fold_slot(bank)
                        for bank in range(2):
                            next_slot()
                            fold_slot(bank)
                        if g == NG - 1:
                            dve.drain()
                            if ffn and c == 0:
                                dve.wait_ge(s_gnn, 2 * (s - 1))
                            dve.tensor_tensor(aggT[:, c * CW:(c + 1) * CW], acc[:, 0, :], acc[:, 1, :],
                                              ALU.max).then_inc(s_agg, 1)
                        if n in (4, 8):
                            reduce_hub(s, (n - 4) // 4, ffn)
                    if ffn:
                        finish(s, k, n)

            def prepare(s, even, n):
                own = some(s * IT, IT)
                if n == 0:
                    if isinstance(s, int):
                        if s in (0, 1, 2, 4):
                            dve.wait_ge(s_x[min(s, 3)], 16 * (1, 1, 2, 0, B - 4)[s])
                    else:
                        dve.wait_ge(s_x[3], 16 * (B - 4))
                    for i in range(IT):
                        dve.bn_stats(stats[:, i, :], xs[:, some(s * IT + i), :].rearrange("p a c -> p (a c)"))
                    dve.drain()
                    for i in range(IT):
                        dve.bn_aggr(mv[:, i, :], stats[:, i, :])
                    dve.drain()
                    dve.tensor_scalar(mv[:, :, 1], mv[:, :, 1], EPS, None, ALU.add).then_inc(s_var1, 1)
                if n == 1:
                    dve.tensor_copy(mean1[:, own], mv[:, :, 0])
                    dve.wait_ge(s_std1, s + 1)
                    newton_rstd(rstd1[:, own], mv[:, :, 1], std[:, :], newton)
                    dve.scalar_tensor_tensor(out=shift1[:, own], in0=mean1[:, own], scalar=-1.0, in1=rstd1[:, own],
                                             op0=ALU.mult, op1=ALU.mult)
                    if isinstance(s, int):
                        if s >= 1:
                            dve.wait_ge(s_tab[1 - even], 16 * ((s - 1) // 2 + 1))
                    else:
                        dve.wait_ge(s_tab[1 - even], (s - even) * 8 + 16 * even)
                    for i in range(IT):
                        t = some(s * IT + i)
                        ins = dve.tensor_scalar(xn[:, i, :], xs[:, t, :].rearrange("p a c -> p (a c)"), mean1[:, t],
                                                rstd1[:, t], ALU.subtract, ALU.mult)
                    ins.then_inc(s_xn, 1)
                if n == 3:
                    dve.wait_ge(s_hi, s + 1)
                    dve.tensor_tensor(rest[:, :, :], xn[:, :, :], xsplit[:, even, 0], ALU.subtract).then_inc(s_rest, 1)
                if n == 5:
                    dve.wait_ge(s_mid, s + 1)
                    dve.tensor_tensor(xsplit[:, even, 2], rest[:, :, :], xsplit[:, even, 1],
                                      ALU.subtract).then_inc(s_split, 1)
                if n == 7:
                    dve.wait_ge(s_cnt, s + 1)
                    for c in range(CHUNKS):
                        dve.tensor_reduce(most[:, some(s * TT + c * TT // CHUNKS, TT // CHUNKS)],
                                          prep_f[c][0:NG + 1, 0:CW].rearrange("p (t i) -> p t i", i=P),
                                          AX_X, ALU.max)
                    dve.drain()
                    step(dve.tensor_reduce(mostc[:, 0, :], most[:, some(s * TT, TT)].rearrange("p (c t) -> p c t", c=CHUNKS),
                                           AX_X, ALU.max))
                    step(dve.tensor_scalar(mostc[:, 1, :], mostc[:, 0, :], 0.5, 0.25, ALU.mult, ALU.add))
                    dve.tensor_scalar(pairs[:, even, :], mostc[:, 1, :], 2.0, float((TOPK + 1) // 2), ALU.max,
                                      ALU.min).then_inc(s_pairs, 1)
                if n >= TT:
                    r = n - TT
                    for h in range(HUBS):
                        if r == 0:
                            a = TT + h
                            dve.wait_ge(s_adj[a % 4], 32 * s + 32)
                            dve.scalar_tensor_tensor(out=score[:, h, :], in0=adj_sb[:, a % 4, :], scalar=0.0,
                                                     in1=down[:, :], op0=ALU.not_equal,
                                                     op1=ALU.mult).then_inc(s_scored, 1)
                    dve.drain()
                    for h in range(HUBS):
                        dve.max(top[:, h, 8 * r:8 * r + 8], score[:, h, :])
                    dve.drain()
                    if r < ROUNDS - 1:
                        for h in range(HUBS):
                            dve.match_replace(score[:, h, :], top[:, h, 8 * r:8 * r + 8], score[:, h, :], 0.0)
                    else:
                        dve.tensor_scalar(floor[:, :], top[:, :, TOPK], 0.0, NEG_BIG, ALU.is_gt, ALU.mult)
                        dve.tensor_scalar(idx[:, :, :], top[:, :, 0:TOPK], -1.0, base[:, some(s)],
                                          ALU.mult, ALU.add).then_inc(s_idx, HUBS)

            def reduce_hub(s, h, ffn):
                b = s - 1
                dve.wait_ge(s_gath, (b * HUBS + h + 1) * (16 * TOPK))
                dve.tensor_reduce(hub_max[:, :], gath[:, :, :].rearrange("p k c -> p c k"), AX_X,
                                  ALU.max).then_inc(s_hubred, 1)
                dve.drain()
                if ffn and h == 0:
                    dve.wait_ge(s_nT, 3 * (s - 1))
                dve.tensor_scalar(hub[:, h, :], hub_max[:, :], floor[:, h:h + 1], None, ALU.max).then_inc(s_hub, 1)

            def fold_weights(m):
                l, e = matrix(m)
                if m == 0:
                    dve.wait_ge(s_wT, 1)
                    dve.tensor_copy(wiT[:, :], ffn_ps[2][:, 0:HID])
                    dve.tensor_copy(woT[:, :, :].rearrange("p j n -> p (j n)"), ffn_ps[2][:, HID:HID + HC * C])
                    step(dve.tensor_copy(biasT[:, :, :].rearrange("p j n -> p (j n)"), ffn_ps[3][:, 0:HC * NB]))
                    for ll in range(L):
                        for j in range(HC):
                            shared = biasT[:, j, L * NE + ll:L * NE + ll + 1]
                            dve.tensor_scalar(bias[:, 0:NE, ll, j], biasT[:, j, ll * NE:(ll + 1) * NE], shared, None,
                                              ALU.add)
                            dve.tensor_copy(bias[:, NE, ll, j:j + 1], shared)
                    dve.drain()
                    dve.wait_ge(s_small, 9 * 16)
                    rf, ok = route_f[:, 0, :], route_f[:, 1, :]
                    step(dve.tensor_copy(rf, route_in[:, :]))
                    step(dve.tensor_scalar(ok, rf, 0.0, None, ALU.is_ge))
                    step(dve.scalar_tensor_tensor(out=ok, in0=rf, scalar=float(NE), in1=ok, op0=ALU.is_lt,
                                                  op1=ALU.mult))
                    step(dve.scalar_tensor_tensor(out=rf, in0=rf, scalar=float(NE), in1=ok, op0=ALU.subtract,
                                                  op1=ALU.mult))
                    dve.tensor_scalar(route[:, :], rf, float(NE), None, ALU.add).then_inc(s_route, 1)
                dve.wait_ge(s_wT, m + 2)
                if m >= NST:
                    dve.wait_ge(s_wstore[m % NST], 16 * (m // NST))
                o = wst[:, m % NST, 0:HC * HID]
                dve.tensor_copy(wst[:, m % NST, HC * HID:WROW], bias[:, e, l, :])
                if m < L:
                    step(dve.tensor_copy(wsI[:, l, :], ffn_ps[m % 2][:, :]))
                    for j in range(HC):
                        c0 = j * HID + j * P
                        dve.tensor_tensor(wsI[:, l, c0:c0 + P], wsI[:, l, c0:c0 + P], ident[:, :], ALU.add)
                    dve.drain()
                    dve.tensor_copy(o, wsI[:, l, :]).then_inc(s_wfold, 1)
                else:
                    dve.tensor_tensor(o, ffn_ps[m % 2][:, :], wsI[:, l, :], ALU.add).then_inc(s_wfold, 1)

            def finish(s, k, n):
                if n == 1:
                    for g in range(2):
                        dve.wait_ge(s_gnn, 2 * k + g + 1)
                        t = some(k * IT + 4 * g, 4)
                        dve.scalar_tensor_tensor(out=x1[:, 4 * g:4 * g + 4, :].rearrange("p t c -> p (t c)"),
                                                 in0=ffn_ps[g][:, :], scalar=0.0,
                                                 in1=xs[:, t, :].rearrange("p t c -> p (t c)"), op0=ALU.max,
                                                 op1=ALU.add)
                    dve.drain()
                    for i in range(IT):
                        dve.bn_stats(st2[:, i, :], x1[:, i, :])
                    dve.drain()
                    for i in range(IT):
                        dve.bn_aggr(mv2[:, i, :], st2[:, i, :])
                    dve.drain()
                    dve.tensor_scalar(mv2[:, :, 1], mv2[:, :, 1], EPS, None, ALU.add).then_inc(s_var2, 1)
                if n == 2:
                    dve.wait_ge(s_std2, k + 1)
                    newton_rstd(r2[:, :], mv2[:, :, 1], std2[:, :], newton)
                    if not (isinstance(s, int) and s == 2):
                        for g in range(2):
                            dve.wait_ge(s_out[g], 16 * k)
                    for i in range(IT):
                        ins = dve.tensor_scalar(h0[:, i, :], x1[:, i, :], mv2[:, i, 0:1], r2[:, i:i + 1],
                                                ALU.subtract, ALU.mult)
                    ins.then_inc(s_h0, 1)
                if n == 8:
                    for g in range(2):
                        dve.wait_ge(s_o, 2 * k + g + 1)
                        dve.tensor_tensor(y[:, 4 * g:4 * g + 4, :].rearrange("p t c -> p (t c)"), ffn_ps[g][:, :],
                                          x1[:, 4 * g:4 * g + 4, :].rearrange("p t c -> p (t c)"),
                                          ALU.add).then_inc(s_y, 1)
            rounds(dve, round_)

            step(dve.tensor_reduce(most_any[:, :], most[:, :], AX_X, ALU.max))
            dve.tensor_scalar(over[:, :], most[:, :], float(TOPK), None, ALU.is_gt)
            dve.tensor_scalar(over_any[:, :], most_any[:, :], float(TOPK), None, ALU.is_gt).then_inc(s_over, 1)

            gathered = dve.alloc_register("gathered")
            dve.reg_mov(gathered, 0)

            def tile_again(t, b, one, dma):
                one_tile = bass.ds(t, 1)
                dve.reg_add(gathered, gathered, 16 * TOPK)
                dve.wait_ge(s_const, CONSTS)
                dve.wait_ge(r_adj, dma)
                step(dve.scalar_tensor_tensor(out=score[:, 0, :], in0=adj_sb[:, 0, :], scalar=0.0, in1=down[:, :],
                                              op0=ALU.not_equal, op1=ALU.mult))
                for r in range(ROUNDS):
                    step(dve.max(top[:, 0, 8 * r:8 * r + 8], score[:, 0, :]))
                    if r < ROUNDS - 1:
                        step(dve.match_replace(score[:, 0, :], top[:, 0, 8 * r:8 * r + 8], score[:, 0, :], 0.0))
                dve.tensor_scalar(floor[:, 0:1], top[:, 0, TOPK:TOPK + 1], 0.0, NEG_BIG, ALU.is_gt, ALU.mult)
                step(dve.tensor_scalar(idx[:, 0, :], top[:, 0, 0:TOPK], -1.0, base[:, bass.ds(b, 1)],
                                       ALU.mult, ALU.add).then_inc(r_idx, 1))
                dve.wait_ge(s_const, CONSTS)
                dve.wait_ge(r_gath, gathered)
                step(dve.tensor_reduce(hub_max[:, :], gath[:, :, :].rearrange("p k c -> p c k"), AX_X, ALU.max))
                step(dve.tensor_scalar(hub[:, 0, :], hub_max[:, :], floor[:, 0:1], None, ALU.max).then_inc(r_hub, 1))
                dve.wait_ge(s_const, CONSTS)
                dve.wait_ge(r_gnn, one)
                step(dve.scalar_tensor_tensor(out=x1[:, 0, :], in0=ffn_ps[0][:, 0:C], scalar=0.0,
                                              in1=xs[:, one_tile, :].rearrange("p t c -> p (t c)"), op0=ALU.max,
                                              op1=ALU.add))
                step(dve.bn_stats(st2[:, 0, :], x1[:, 0, :]))
                step(dve.bn_aggr(mv2[:, 0, :], st2[:, 0, :]))
                step(dve.tensor_scalar(mv2[:, 0, 1:2], mv2[:, 0, 1:2], EPS, None, ALU.add).then_inc(r_var, 1))
                dve.wait_ge(s_const, CONSTS)
                dve.wait_ge(r_std, one)
                newton_rstd(r2[:, 0:1], mv2[:, 0, 1:2], std2[:, 0:1], newton[:, :, 0:1])
                step(dve.tensor_scalar(h0[:, 0, :], x1[:, 0, :], mv2[:, 0, 0:1], r2[:, 0:1], ALU.subtract,
                                       ALU.mult).then_inc(r_h0, 1))
                dve.wait_ge(s_const, CONSTS)
                dve.wait_ge(r_o, one)
                step(dve.tensor_tensor(y[:, 0, :], ffn_ps[3][:, 0:C], x1[:, 0, :], ALU.add).then_inc(r_y, 1))
            again(dve, tile_again)


_INS = ['x', 'adj', 'L0_gnn_W', 'L0_gnn_b', 'L0_ffn_route_id', 'L0_ffn_Wi', 'L0_ffn_bi', 'L0_ffn_Wr', 'L0_ffn_br',
        'L0_ffn_Ws', 'L0_ffn_bs', 'L0_ffn_Wo', 'L0_ffn_bo']
_OUTS = [((8, 1024, 128), 'float32')]


def kernel(**inputs):
    import numpy as _np
    import concourse.bacc as _bacc
    from concourse import mybir as _mybir
    from concourse.bass_utils import run_bass_kernel_spmd as _run

    nc = _bacc.Bacc("TRN2", target_bir_lowering=False, num_devices=1)
    arrays, args = {}, []
    for name in _INS:
        a = _np.ascontiguousarray(inputs[name])
        arrays[f"in_{name}_dram"] = a
        args.append(nc.dram_tensor(f"in_{name}_dram", a.shape, _mybir.dt.from_np(a.dtype), kind="ExternalInput").ap())
    for i, (shape, dtype) in enumerate(_OUTS):
        dt = _mybir.dt.from_np(_np.dtype(dtype))
        args.append(nc.dram_tensor(f"out_{i}_dram", shape, dt, kind="ExternalOutput").ap())
    gnn_ffn_program(nc, *args)
    r = _run(nc, [arrays], core_ids=[0])
    got = tuple(r.results[0][f"out_{i}_dram"] for i in range(len(_OUTS)))
    return got[0]
```

```python
from contextlib import ExitStack

import concourse.bass as bass
from concourse import mybir

F32 = mybir.dt.float32
BF16 = mybir.dt.bfloat16
I32 = mybir.dt.int32
ALU = mybir.AluOpType
ACT = mybir.ActivationFunctionType
AX_X = mybir.AxisListType.X

P = 128
TOPK = 25
ROUNDS = 4
EPS = 1e-5
ROUNDER = 1.5 * 2 ** 23
NEG_BIG = -3.0e38
HUBS = 2
CHUNKS = 2
POS = 10
GROUPS = [(0, 1), (1, 1), (2, 2), (4, 2), (6, 2)]
SPLITS = 3


def gnn_ffn_program(nc, x, adj, gnn_W, gnn_b, route_id, Wi, bi, Wr, br, Ws, bs, Wo, bo, out):
    B, N, C = x.shape
    IT = N // P
    T = B * IT
    TT = IT - HUBS
    CW = TT * P // CHUNKS
    HID = Wi.shape[0]
    HC = HID // P
    L, NE = Wr.shape[0], Wr.shape[1]
    E1 = NE + 1
    NB = L * NE + L + 1
    NG = len(GROUPS)
    BANK = 512
    SMALL = 7 + 2 * SPLITS
    TABROW = N + 1
    WROW = HC * HID + HC
    NW = L * E1
    ZROWS = 16
    ZEROS = B * N // (P * ZROWS) + 1
    CONSTS = NG + 7
    ORDER = [2, 3, 4, 5, 0, 1, 6, 7]
    SCORE_AT, TOP_AT, REDUCE_AT = 3, (4, 6, 7, 9), (5, 8)
    IN_AT, LAYER_AT, OUT_AT = (4, 5), [{6: range(0, IT)}, {7: range(0, IT // 2), 8: range(IT // 2, IT)}], 9
    RANK_BEFORE = {7: [0], 8: [2], 9: [5]}
    RANK_AFTER = {7: [1], 8: [3, 4], 9: [6, 7]}
    assert POS == CHUNKS * NG and HC == 2 and L == 2

    x_t = x.rearrange("b (t p) c -> b p t c", p=P)
    adj_t = adj.rearrange("b (t p) n -> (b t) p n", p=P)
    out_t = out.rearrange("b (t p) c -> b p t c", p=P)
    out_rows = out.rearrange("b (t p) c -> (b t) p c", p=P)
    table = nc.dram_tensor("feature_table", [B * TABROW, C], F32, kind="Internal").ap()
    table_b = table.rearrange("(b r) c -> b r c", b=B)
    folded = nc.dram_tensor("folded_weights", [L * E1, P, WROW], F32, kind="Internal").ap()
    wr_t = Wr.rearrange("l e (j p) d -> (l e) p j d", p=P)
    ws_t = Ws.rearrange("l s (j p) d -> (l s) p j d", p=P)

    with ExitStack() as ctx:
        def sb(name, shape, dt=F32):
            return ctx.enter_context(nc.sbuf_tensor(name, shape, dt))

        def pb(name, shape, dt=F32):
            return ctx.enter_context(nc.psum_tensor(name, shape, dt))

        def sem(name):
            return ctx.enter_context(nc.semaphore(name))

        ident = sb("ident", [P, P])
        identb = sb("identb", [P, P], BF16)
        before = sb("before", [P, P], BF16)
        onesb = sb("onesb", [P, P], BF16)
        pick = sb("pick", [P, IT, NG + 1], BF16)
        down = sb("down", [P, N])
        ranks = sb("ranks", [P, 32])
        base = sb("base", [P, B])
        gw = sb("gw", [P, 2, C])
        bias_rows = sb("bias_rows", [SPLITS, 2, BANK // C, C], BF16)
        wiT = sb("wiT", [P, HID])
        woT = sb("woT", [P, HC, C])
        biasT = sb("biasT", [P, HC, NB])
        bias = sb("bias", [P, E1, L, HC])
        route_f = sb("route_f", [1, 2, T])
        route = sb("route", [1, T], I32)
        route_in = sb("route_in", [1, T], I32)

        xs = sb("xs", [P, T, C])
        rstd1 = sb("rstd1", [P, T])
        shift1 = sb("shift1", [P, T])
        stats = sb("stats", [P, IT, 6])
        mv = sb("mv", [P, IT, 2])
        std = sb("std", [P, IT])
        newton = sb("newton", [P, 2, IT])
        xn = sb("xn", [P, IT, C])
        rest = sb("rest", [P, IT, C])
        xsplit = sb("xsplit", [P, 2, SPLITS, IT, C], BF16)

        adj_sb = sb("adj_sb", [P, 4, N], I32)
        mask = sb("mask", [P, 2, N], BF16)
        at = sb("at", [P, IT, TT * P], BF16)
        rank = sb("rank", [P, 2, IT, TT * P], BF16)
        onehot = sb("onehot", [P, 2, 2, CW], BF16)
        acc = sb("acc", [P, CHUNKS, 2, CW])
        aggT = sb("aggT", [P, TT * P])
        most = sb("most", [NG + 1, B * TT])
        most_any = sb("most_any", [NG + 1, 1])
        over = sb("over", [NG + 1, B * TT], I32)
        over_any = sb("over_any", [NG + 1, 1], I32)
        mostc = sb("mostc", [NG + 1, 2, CHUNKS])
        pairs = sb("pairs", [NG + 1, 2, CHUNKS], I32)

        score = sb("score", [P, HUBS, N])
        top = sb("top", [P, HUBS, 8 * ROUNDS])
        idx = sb("idx", [P, HUBS, TOPK], I32)
        floor = sb("floor", [P, HUBS])
        gath = sb("gath", [P, TOPK, C])
        hub_max = sb("hub_max", [P, C])
        hub = sb("hub", [P, HUBS, C])
        hubT = sb("hubT", [P, HUBS, C])

        xnf = sb("xnf", [P, IT, C])
        xnT = sb("xnT", [P, IT, C])
        x1 = sb("x1", [P, IT, C])
        st2 = sb("st2", [P, IT, 6])
        mv2 = sb("mv2", [P, IT, 2])
        std2 = sb("std2", [P, IT])
        r2 = sb("r2", [P, IT])
        shift2 = sb("shift2", [P, IT])
        h0 = sb("h0", [P, IT, C])
        h0T = xnT
        hT = sb("hT", [P, 2, HC, IT, P])
        wst = sb("wst", [P, IT, WROW])
        y = h0
        bias_raw, bias_rest, bias_last, bias_sum = (
            score[0:SPLITS, 0, i * 2 * C:(i + 1) * 2 * C].rearrange("p (v c) -> p v c", v=2) for i in range(4))
        wsI = x1[:, :, :].rearrange("p t c -> p (t c)").rearrange("p (l w) -> p l w", l=L)
        w_in = [half for whole in (xnf, h0) for half in (
            whole[:, 0:IT // 2, :].rearrange("p t c -> p (t c)").rearrange("p (j d) -> p j d", j=HC),
            whole[:, IT // 2:IT, :].rearrange("p t c -> p (t c)").rearrange("p (j d) -> p j d", j=HC))]
        wi_in = xnT[:, 0:HC, :]
        wo_in = xnT[:, HC:2 * HC, :].rearrange("p a c -> p (a c)")
        bias_in = xnT[0:NB, 2 * HC:3 * HC, :].rearrange("p a c -> p (a c)")
        NIN = 4
        NST = 4

        slot_ps = [pb(f"slot_ps{i}", [P, 512]) for i in range(2)]
        prep_ps = [pb(f"prep_ps{i}", [P, 1024], BF16) for i in range(2)]
        ffn_ps = [pb(f"ffn_ps{i}", [P, 512]) for i in range(4)]
        prep_f = [p[:, :].bitcast(F32) for p in prep_ps]

        s_memset = sem("s_memset")
        s_const = sem("s_const")
        s_zero = sem("s_zero")
        s_x = [sem(f"s_x{b}") for b in range(4)]
        s_small = sem("s_small")
        s_wload = [sem(f"s_wload{i}") for i in range(NIN)]
        s_bias = sem("s_bias")
        s_wT = sem("s_wT")
        s_wfold = sem("s_wfold")
        s_wstore = [sem(f"s_wstore{i}") for i in range(NST)]
        s_route = sem("s_route")
        s_var1 = sem("s_var1")
        s_std1 = sem("s_std1")
        s_norm1 = sem("s_norm1")
        s_norm2 = sem("s_norm2")
        s_xn = sem("s_xn")
        s_hi = sem("s_hi")
        s_rest = sem("s_rest")
        s_mid = sem("s_mid")
        s_split = sem("s_split")
        s_tab = [sem(f"s_tab{i}") for i in range(2)]
        s_adj = [sem(f"s_adj{i}") for i in range(4)]
        s_scored = sem("s_scored")
        s_mask = sem("s_mask")
        s_tr = sem("s_tr")
        s_at = sem("s_at")
        s_cnt = sem("s_cnt")
        s_pairs = sem("s_pairs")
        s_rank = sem("s_rank")
        s_q = sem("s_q")
        s_onehot = sem("s_onehot")
        s_slot = sem("s_slot")
        s_max = sem("s_max")
        s_clear = sem("s_clear")
        s_agg = sem("s_agg")
        s_idx = sem("s_idx")
        s_gath = sem("s_gath")
        s_hubred = sem("s_hubred")
        s_hub = sem("s_hub")
        s_xnf = sem("s_xnf")
        s_nT = sem("s_nT")
        s_nTc = sem("s_nTc")
        s_gnn = sem("s_gnn")
        s_var2 = sem("s_var2")
        s_std2 = sem("s_std2")
        s_h0 = sem("s_h0")
        s_h0T = sem("s_h0T")
        s_h0c = sem("s_h0c")
        s_in = sem("s_in")
        s_inr = sem("s_inr")
        s_l = [sem(f"s_l{l}") for l in range(L)]
        s_r = [sem(f"s_r{l}") for l in range(L)]
        s_w = [sem(f"s_w{i}") for i in range(IT)]
        s_o = sem("s_o")
        s_y = sem("s_y")
        s_out = [sem(f"s_out{i}") for i in range(2)]

        s_over = sem("s_over")
        r_adj = sem("r_adj")
        r_w = [sem(f"r_w{l}") for l in range(L)]
        r_idx = sem("r_idx")
        r_gath = sem("r_gath")
        r_hub = sem("r_hub")
        r_xn = sem("r_xn")
        r_T = sem("r_T")
        r_Tc = sem("r_Tc")
        r_gnn = sem("r_gnn")
        r_var = sem("r_var")
        r_std = sem("r_std")
        r_h0 = sem("r_h0")
        r_h0T = sem("r_h0T")
        r_h0c = sem("r_h0c")
        r_in = sem("r_in")
        r_inr = sem("r_inr")
        r_l = [sem(f"r_l{l}") for l in range(L)]
        r_r = [sem(f"r_r{l}") for l in range(L)]
        r_o = sem("r_o")
        r_y = sem("r_y")
        r_stored = sem("r_stored")

        block = ctx.enter_context(nc.Block())

        def rounds(eng, body):
            body(0, 0, True, False, False)
            body(1, 1, True, True, False)
            body(2, 0, True, True, True)
            body(3, 1, True, True, True)
            with eng.Fori(2, B // 2) as q:
                body(q * 2, 0, True, True, True)
                body(q * 2 + 1, 1, True, True, True)
            body(B, 0, False, True, True)
            body(B + 1, 1, False, False, True)

        def again(eng, body):
            one = eng.alloc_register(f"again_{eng.engine.name}")
            dma = eng.alloc_register(f"again16_{eng.engine.name}")
            eng.reg_mov(one, 0)
            eng.reg_mov(dma, 0)
            eng.wait_ge(s_over, 1)
            some_over = eng.value_load(over_any[NG:NG + 1, 0:1], min_val=0, max_val=1)
            with eng.If(some_over > 0):
                with eng.Fori(0, B) as b:
                    with eng.Fori(0, TT) as i:
                        is_over = eng.value_load(over[NG:NG + 1, bass.ds(b * TT + i, 1)], min_val=0, max_val=1)
                        with eng.If(is_over > 0):
                            eng.reg_add(one, one, 1)
                            eng.reg_add(dma, dma, 16)
                            body(b * IT + HUBS + i, b, one, dma)

        def some(t, n=1):
            return slice(t, t + n) if isinstance(t, int) else bass.ds(t, n)

        def weights_of(s, n):
            if not isinstance(s, int) or s > 1:
                return []
            return [m for m in range(2 * (POS * s + n), 2 * (POS * s + n) + 2) if m < NW]

        def matrix(m):
            return (m, NE) if m < L else ((m - L) // NE, (m - L) % NE)

        @block.sync
        def _(sp):
            def load_x(first, many, signal):
                for b in range(first, first + many):
                    sp.dma_start(xs[:, b * IT:(b + 1) * IT, :], x_t[b]).then_inc(s_x[signal], 16)

            load_x(0, 1, 0)
            sp.dma_start(wi_in, Wi.rearrange("(j p) d -> p j d", p=P)).then_inc(s_small, 16)
            sp.dma_start(wo_in, Wo).then_inc(s_small, 16)
            sp.dma_start(bias_in[0:L * NE], br.rearrange("l e h -> (l e) h")).then_inc(s_small, 16)
            sp.dma_start(bias_in[L * NE:L * NE + L], bs.rearrange("l s h -> (l s) h")).then_inc(s_small, 16)
            sp.dma_start(bias_in[NB - 1:NB], bi.rearrange("(a n) -> a n", a=1)).then_inc(s_small, 16)
            sp.dma_start(gw[:, :, :], gnn_W.rearrange("(j p) d -> p j d", p=P)).then_inc(s_small, 16)
            for p in range(SPLITS):
                for which, vector in enumerate((gnn_b, bo)):
                    sp.dma_start(bias_raw[p:p + 1, which, :], vector.rearrange("(a n) -> a n", a=1)
                                 ).then_inc(s_small, 16)
            sp.dma_start(route_in[:, :], route_id.rearrange("(a n) -> a n", a=1)).then_inc(s_small, 16)
            for m in range(NIN):
                sp.dma_start(w_in[m], ws_t[m] if m < L else wr_t[m - L]).then_inc(s_wload[m], 16)
            for a in range(4):
                sp.dma_start(adj_sb[:, a, :], adj_t[ORDER[a]]).then_inc(s_adj[a], 16)
            load_x(1, 1, 1)

            def round_(s, even, prep, slots, ffn):
                k = s - 2
                for n in range(POS):
                    if isinstance(s, int) and (s, n) == (0, 5):
                        load_x(2, 2, 2)
                    if isinstance(s, int) and (s, n) == (1, 1):
                        load_x(4, B - 4, 3)
                    for q in (range(4) if n == 0 else [n + 3] if n < 5 else []):
                        if not prep or (isinstance(s, int) and s == 0 and q < 4):
                            continue
                        if q >= 2:
                            sp.wait_ge(s_mask, s * TT + q - 3)
                        else:
                            sp.wait_ge(s_scored, s * HUBS + q - 1)
                        tile = ORDER[q]
                        sp.dma_start(adj_sb[:, q % 4, :], adj_t[s * IT + tile] if isinstance(s, int) else
                                     adj_t[some(s * IT + tile)].rearrange("a p n -> (a p) n")
                                     ).then_inc(s_adj[q % 4], 16)
                    if ffn and n == 0:
                        for i in range(IT):
                            e = sp.value_load(route[0:1, some(k * IT + i)], min_val=0, max_val=NE)
                            if i == 0 and not (isinstance(s, int) and s == 2):
                                sp.wait_ge(s_r[1], k * IT)
                            sp.dma_start(wst[:, i, :], folded[bass.ds(e, 1)].rearrange("a p w -> (a p) w")
                                         ).then_inc(s_w[i], 16)
                    if prep and n == 2:
                        if isinstance(s, int) and s == 0:
                            sp.wait_ge(s_zero, 16 * ZEROS)
                        sp.wait_ge(s_xn, s + 1)
                        sp.dma_start(table_b[some(s), 0:N, :].rearrange("a (t p) c -> (a p) t c", p=P), xn[:, :, :]
                                     ).then_inc(s_tab[even], 16)
                    for m in weights_of(s, n):
                        if m + NIN < NW:
                            sp.wait_ge(s_wT, m + 2)
                            sp.dma_start(w_in[m % NIN], ws_t[m + NIN] if m + NIN < L else wr_t[m + NIN - L]
                                         ).then_inc(s_wload[m % NIN], 16)
                    if ffn and n == 6:
                        for i in range(IT):
                            e = sp.value_load(route[0:1, some(k * IT + i)], min_val=0, max_val=NE)
                            sp.wait_ge(s_r[0], k * IT + i + 1)
                            sp.dma_start(wst[:, i, :], folded[bass.ds(e + E1, 1)].rearrange("a p w -> (a p) w")
                                         ).then_inc(s_w[i], 16)

            def all_rounds(s, even, prep, slots, ffn):
                round_(s, even, prep, slots, ffn)
                if isinstance(s, int) and s == 1:
                    sp.wait_ge(s_route, 1)
                    for i in range(NST):
                        sp.wait_ge(s_wstore[i], 16 * len(range(i, NW, NST)))
            rounds(sp, all_rounds)

            for g in range(2):
                sp.wait_ge(s_out[g], 16 * B)

            def tile_again(t, b, one, dma):
                sp.dma_start(adj_sb[:, 0, :], adj_t[bass.ds(t, 1)].rearrange("a p n -> (a p) n")).then_inc(r_adj, 16)
                e = sp.value_load(route[0:1, bass.ds(t, 1)], min_val=0, max_val=NE)
                for l in range(L):
                    sp.dma_start(wst[:, l, :], folded[bass.ds(e + l * E1, 1)].rearrange("a p w -> (a p) w")
                                 ).then_inc(r_w[l], 16)
                sp.wait_ge(s_const, CONSTS)
                sp.wait_ge(r_y, one)
                sp.dma_start(out_rows[bass.ds(t, 1)].rearrange("a p c -> (a p) c"), y[:, 0, :]).then_inc(r_stored, 16)
                sp.wait_ge(s_const, CONSTS)
                sp.wait_ge(r_stored, dma)
            again(sp, tile_again)

        @block.gpsimd
        def _(pool):
            pool.memset(ident[:, :], 0.0).then_inc(s_memset, 1)
            pool.memset(onesb[:, :], 1.0).then_inc(s_memset, 1)
            pool.memset(pick[:, :, :], 0.0).then_inc(s_memset, 1)
            pool.wait_ge(s_memset, 3)
            pool.affine_select(out=ident[:, :], in_=ident[:, :], compare_op=ALU.not_equal, fill=1.0,
                               base=0, pattern=[[-1, P]], channel_multiplier=1).then_inc(s_memset, 1)
            pool.affine_select(out=before[:, :], in_=onesb[:, :], compare_op=ALU.is_gt, fill=0.0,
                               base=0, pattern=[[1, P]], channel_multiplier=-1).then_inc(s_memset, 1)
            pool.wait_ge(s_memset, 5)
            pool.affine_select(out=before[:, :], in_=before[:, :], compare_op=ALU.not_equal, fill=256.0,
                               base=0, pattern=[[1, P]], channel_multiplier=-1).then_inc(s_const, 1)
            pool.tensor_copy(identb[:, :], ident[:, :]).then_inc(s_const, 1)
            for g, (first, many) in enumerate(GROUPS):
                pool.memset(pick[:, first:first + many, g:g + 1], 1.0).then_inc(s_const, 1)
            pool.memset(pick[:, :, NG:NG + 1], 1.0).then_inc(s_const, 1)
            pool.iota(down[:, :], [[-1, N]], N, channel_multiplier=0,
                      allow_small_or_imprecise_dtypes=True).then_inc(s_const, 1)
            pool.iota(ranks[:, :], [[1, 32]], 1, channel_multiplier=0,
                      allow_small_or_imprecise_dtypes=True).then_inc(s_const, 1)
            pool.iota(base[:, :], [[TABROW, B]], N, channel_multiplier=0,
                      allow_small_or_imprecise_dtypes=True).then_inc(s_const, 1)
            pool.memset(gath[:, 0:ZROWS, :], 0.0).then_inc(s_const, 1)
            pool.wait_ge(s_const, CONSTS)
            for b in range(4):
                pool.wait_ge(s_adj[b], 16)
                pool.wait_ge(s_wload[b], 16)
            for z in range(0, B * N, P * ZROWS):
                pool.dma_start(table[z:z + P * ZROWS].rearrange("(p t) c -> p t c", p=P), gath[:, 0:ZROWS, :]
                               ).then_inc(s_zero, 16)
            pool.dma_start(table[B * N:B * TABROW], gath[0:B, 0, :]).then_inc(s_zero, 16)
            pool.wait_ge(s_zero, 16 * ZEROS)
            hubs_begun, hubs_done, tables, split_graphs = (
                pool.alloc_register(r) for r in ("hubs_begun", "hubs_done", "tables", "split_graphs"))
            for counter in (hubs_begun, hubs_done, tables, split_graphs):
                pool.reg_mov(counter, 0)

            def first_rest(par):
                pool.reg_add(split_graphs, split_graphs, 1)
                pool.wait_ge(s_const, CONSTS)
                pool.wait_ge(s_hi, split_graphs)
                pool.tensor_tensor(rest[:, :, :], xn[:, :, :], xsplit[:, par, 0],
                                   ALU.subtract).then_inc(s_rest, 1)

            def second_rest(par):
                pool.wait_ge(s_const, CONSTS)
                pool.wait_ge(s_mid, split_graphs)
                pool.tensor_tensor(xsplit[:, par, 2], rest[:, :, :], xsplit[:, par, 1],
                                   ALU.subtract).then_inc(s_split, 1)

            def graph(par, first, last):
                if par == 0:
                    pool.reg_add(tables, tables, 16)
                for h in range(HUBS):
                    skip = first and h == 0
                    pool.reg_add(hubs_begun, hubs_begun, 1)
                    if not skip:
                        pool.reg_add(hubs_done, hubs_done, 1)
                    pool.wait_ge(s_const, CONSTS)
                    pool.wait_ge(s_idx, hubs_begun)
                    pool.wait_ge(s_tab[par], tables)
                    if not skip:
                        pool.wait_ge(s_hubred, hubs_done)
                    for j in range(TOPK):
                        pool.indirect_dma_start(gath[:, j, :], None, table,
                                                bass.IndirectOffsetOnAxis(ap=idx[:, h, j:j + 1], axis=0)
                                                ).then_inc(s_gath, 16)
                    if not last:
                        if h == 0:
                            first_rest(1 - par)
                        else:
                            second_rest(1 - par)

            first_rest(0)
            second_rest(0)
            graph(0, True, False)
            graph(1, False, False)
            with pool.Fori(1, B // 2 - 1):
                graph(0, False, False)
                graph(1, False, False)
            graph(0, False, False)
            graph(1, False, True)

            def tile_again(t, b, one, dma):
                pool.wait_ge(s_const, CONSTS)
                pool.wait_ge(r_idx, one)
                for j in range(TOPK):
                    pool.indirect_dma_start(gath[:, j, :], None, table,
                                            bass.IndirectOffsetOnAxis(ap=idx[:, 0, j:j + 1], axis=0)
                                            ).then_inc(r_gath, 16)
            again(pool, tile_again)

        @block.scalar
        def _(act):
            act.wait_ge(s_const, CONSTS)

            graphs, graphs_before, tables, transposed = (act.alloc_register(r) for r in (
                "act_graphs", "act_graphs_before", "act_tables", "act_transposed"))
            for counter, start in ((graphs, 1), (graphs_before, 0), (tables, 16), (transposed, 3)):
                act.reg_mov(counter, start)

            def normalise(act, to, t):
                return act.activation(to, xs[:, t, :].rearrange("p a c -> p (a c)"), ACT.Identity,
                                      bias=shift1[:, t], scale=rstd1[:, t])

            def clear(c):
                act.activation(acc[:, c].rearrange("p b i -> p (b i)"), down[:, 0:2 * CW], ACT.Copy,
                               scale=0.0).then_inc(s_clear, 1)
            for c in range(CHUNKS):
                clear(c)

            def rank_tiles(s, even, tiles, ffn):
                for jt in tiles:
                    for c in range(CHUNKS):
                        act.wait_ge(s_rank, 2 * IT * s + 2 * jt + c + 1)
                        if jt == 0 and c == 0 and ffn:
                            act.wait_ge(s_agg, CHUNKS * (s - 1))
                        act.activation(rank[:, even, jt, c * CW:(c + 1) * CW], prep_f[c][:, 0:CW],
                                       ACT.Copy, bias=-255.0).then_inc(s_q, 1)

            def round_(s, even, prep, slots, ffn):
                k = s - 2
                for n in range(POS):
                    for m in weights_of(s, n):
                        l, e = matrix(m)
                        act.wait_ge(s_wfold, m + 1)
                        act.dma_start(folded[l * E1 + e], wst[:, m % NST, :]).then_inc(s_wstore[m % NST], 16)
                    if slots and n == POS - 1:
                        if ffn:
                            act.wait_ge(s_nT, transposed)
                            act.reg_add(transposed, transposed, 3)
                        elif isinstance(s, int):
                            act.wait_ge(s_wT, NW + 1)
                        for i in range(IT):
                            ins = normalise(act, xnf[:, i, :], some((s - 1) * IT + i))
                        ins.then_inc(s_xnf, 1)
                    if ffn and n == 2:
                        act.wait_ge(s_var2, k + 1)
                        act.activation(std2[:, :], mv2[:, :, 1], ACT.Sqrt).then_inc(s_std2, 1)
                    if ffn and n == 3:
                        if not (isinstance(s, int) and s == 2):
                            for g in range(2):
                                act.wait_ge(s_out[g], 16 * k)
                        act.wait_ge(s_norm2, k + 1)
                        for i in range(IT):
                            ins = act.activation(h0[:, i, :], x1[:, i, :], ACT.Identity, bias=shift2[:, i:i + 1],
                                                 scale=r2[:, i:i + 1])
                        ins.then_inc(s_h0, 1)
                    if prep:
                        if n < TT:
                            q = ORDER.index(n + HUBS)
                            act.wait_ge(s_adj[q % 4], 32 * s + 16 * (q // 4 + 1))
                            if n >= 2 or not (isinstance(s, int) and s == 0):
                                act.wait_ge(s_tr, s * TT + n - 1)
                            act.activation(mask[:, n % 2, :], adj_sb[:, q % 4, :], ACT.Sign).then_inc(s_mask, 1)
                        if n == 0:
                            act.wait_ge(s_var1, s + 1)
                            act.activation(std[:, :], mv[:, :, 1], ACT.Sqrt).then_inc(s_std1, 1)
                        if n == 1:
                            first = isinstance(s, int) and s == 0
                            act.wait_ge(s_norm1, graphs)
                            if not first:
                                act.wait_ge(s_rest, graphs_before)
                                act.wait_ge(s_tab[1 - even], tables)
                            act.reg_add(graphs, graphs, 1)
                            act.reg_add(graphs_before, graphs_before, 1)
                            if not even and not first:
                                act.reg_add(tables, tables, 16)
                            for i in range(IT):
                                ins = normalise(act, xn[:, i, :], some(s * IT + i))
                            ins.then_inc(s_xn, 1)
                        if n == 2:
                            act.wait_ge(s_xn, s + 1)
                            if ffn:
                                act.wait_ge(s_agg, CHUNKS * (s - 1))
                            act.activation(xsplit[:, even, 0], xn[:, :, :], ACT.Copy).then_inc(s_hi, 1)
                        if n == 4:
                            act.wait_ge(s_rest, s + 1)
                            act.activation(xsplit[:, even, 1], rest[:, :, :], ACT.Copy).then_inc(s_mid, 1)
                    if ffn:
                        if n == 0:
                            for g in range(3):
                                act.wait_ge(s_nT, 3 * k + g + 1)
                                if g < 2:
                                    act.activation(xnT[:, 4 * g:4 * g + 4, :].rearrange("p t c -> p (t c)"),
                                                   ffn_ps[g][:, :], ACT.Copy).then_inc(s_nTc, 1)
                                else:
                                    act.activation(hubT[:, :, :].rearrange("p t c -> p (t c)"),
                                                   ffn_ps[2][:, 0:HUBS * C], ACT.Copy).then_inc(s_nTc, 1)
                        if n == 3:
                            for g in range(2):
                                act.wait_ge(s_h0T, 2 * k + g + 1)
                                act.activation(h0T[:, 4 * g:4 * g + 4, :].rearrange("p t c -> p (t c)"),
                                               ffn_ps[g][:, :], ACT.Copy).then_inc(s_h0c, 1)
                        if n in IN_AT:
                            g = IN_AT.index(n)
                            act.wait_ge(s_in, 2 * k + g + 1)
                            for j in range(HC):
                                ins = act.activation(hT[:, 0, j, 4 * g:4 * g + 4, :].rearrange("p t c -> p (t c)"),
                                                     ffn_ps[2 * (1 - g) + j][:, :], ACT.Relu,
                                                     bias=biasT[:, j, NB - 1:NB])
                            ins.then_inc(s_inr, 1)
                        for l in range(L):
                            for i in LAYER_AT[l].get(n, []):
                                act.wait_ge(s_l[l], k * IT + i + 1)
                                for j in range(HC):
                                    c0 = (i // 4) * HID + j * P
                                    ins = act.activation(hT[:, 1 - l, j, i, :], ffn_ps[i % 4][:, c0:c0 + P],
                                                         ACT.Relu, bias=wst[:, i, HC * HID + j:HC * HID + j + 1])
                                ins.then_inc(s_r[l], 1)
                    if prep:
                        rank_tiles(s, even, RANK_BEFORE.get(n, []), ffn)
                        if n < TT:
                            act.wait_ge(s_tr, s * TT + n + 1)
                            if n == 0 and not (isinstance(s, int) and s == 0):
                                act.wait_ge(s_rank, 2 * IT * s)
                            act.activation(at[:, :, n * P:(n + 1) * P],
                                           prep_ps[n % 2][:, :].rearrange("p (j i) -> p j i", j=IT),
                                           ACT.Square).then_inc(s_at, 1)
                        rank_tiles(s, even, RANK_AFTER.get(n, []), ffn)
                    if slots and n == NG + 1:
                        act.wait_ge(s_agg, CHUNKS * (s - 1) + 1)
                        clear(0)
                    if slots and ffn and n == 1:
                        act.wait_ge(s_agg, CHUNKS * (s - 1))
                        clear(1)
                    if ffn and n == OUT_AT:
                        for g in range(2):
                            act.wait_ge(s_y, k * 2 + g + 1)
                            act.dma_start(out_t[some(k), :, 4 * g:4 * g + 4, :].rearrange("a p t c -> (a p) t c"),
                                          y[:, 4 * g:4 * g + 4, :]).then_inc(s_out[g], 16)
            rounds(act, round_)

            def tile_again(t, b, one, dma):
                one_tile = bass.ds(t, 1)
                act.wait_ge(s_const, CONSTS)
                act.wait_ge(r_adj, dma)
                normalise(act, xnf[:, 0, :], one_tile).then_inc(r_xn, 1)
                act.wait_ge(s_const, CONSTS)
                act.wait_ge(r_T, one)
                act.activation(xnT[:, 0, :], ffn_ps[0][:, 0:C], ACT.Copy)
                act.activation(hubT[:, 0, :], ffn_ps[1][:, 0:C], ACT.Copy).then_inc(r_Tc, 1)
                act.wait_ge(s_const, CONSTS)
                act.wait_ge(r_var, one)
                act.activation(std2[:, 0:1], mv2[:, 0, 1:2], ACT.Sqrt).then_inc(r_std, 1)
                act.wait_ge(s_const, CONSTS)
                act.wait_ge(r_h0T, one)
                act.activation(h0T[:, 0, :], ffn_ps[1][:, 0:C], ACT.Copy).then_inc(r_h0c, 1)
                act.wait_ge(s_const, CONSTS)
                act.wait_ge(r_in, one)
                for j in range(HC):
                    ins = act.activation(hT[:, 0, j, 0, :], ffn_ps[2][:, j * P:(j + 1) * P], ACT.Relu,
                                         bias=biasT[:, j, NB - 1:NB])
                ins.then_inc(r_inr, 1)
                for l in range(L):
                    act.wait_ge(s_const, CONSTS)
                    act.wait_ge(r_l[l], one)
                    for j in range(HC):
                        ins = act.activation(hT[:, 1 - l, j, 0, :], ffn_ps[l][:, j * P:(j + 1) * P], ACT.Relu,
                                             bias=wst[:, l, HC * HID + j:HC * HID + j + 1])
                    ins.then_inc(r_r[l], 1)
            again(act, tile_again)

        @block.tensor
        def _(pe):
            pe.wait_ge(s_const, CONSTS)
            slots_done = pe.alloc_register("slots_done")
            pe.reg_mov(slots_done, 0)

            def start_with_bias(bank, which):
                pe.matmul(bank, onesb[0:SPLITS, :], bias_rows[:, which].rearrange("p t c -> p (t c)"),
                          start=True, stop=False)

            def slot(even, first, many, bank):
                pe.reg_add(slots_done, slots_done, 1)
                pe.wait_ge(s_onehot, slots_done)
                pe.wait_ge(s_max, slots_done)
                for j in range(many):
                    for p in range(SPLITS):
                        mm = pe.matmul(slot_ps[bank][:, 0:CW], xsplit[:, even, p, first + j, :],
                                       onehot[:, bank, j, :], start=(j == 0 and p == 0),
                                       stop=(j == many - 1 and p == SPLITS - 1))
                mm.then_inc(s_slot, 1)

            def rank_tiles(s, tiles):
                for jt in tiles:
                    second = [f for f, many in GROUPS if many == 2 and f + 1 == jt]
                    for c in range(CHUNKS):
                        if jt == 0:
                            pe.wait_ge(s_pairs, s + 1)
                        else:
                            pe.wait_ge(s_q, 2 * IT * s + 2 * jt + c - 1)
                        cols = slice(c * CW, (c + 1) * CW)
                        mm = pe.matmul(prep_f[c][:, 0:CW], before[:, :], at[:, jt, cols],
                                       start=True, stop=not second)
                        if second:
                            mm = pe.matmul(prep_f[c][:, 0:CW], onesb[:, :], at[:, jt - 1, cols],
                                           start=False, stop=True)
                        mm.then_inc(s_rank, 1)

            def round_(s, even, prep, slots, ffn):
                k = s - 2
                if slots:
                    pe.wait_ge(s_const, CONSTS)
                    pe.wait_ge(s_pairs, s)
                    pe.wait_ge(s_split, s)
                    for bank in range(2):
                        slot(1 - even, *GROUPS[0], bank)
                for n in range(POS):
                    if isinstance(s, int) and s == 0 and n == 0:
                        pe.wait_ge(s_small, SMALL * 16)
                        for j in range(HC):
                            pe.transpose(ffn_ps[2][:, j * P:(j + 1) * P], wi_in[:, j, :], ident[:, :])
                        for j in range(HC):
                            pe.transpose(ffn_ps[2][:, (HC + j) * P:(HC + j + 1) * P], wo_in[:, j * P:(j + 1) * P],
                                         ident[:, :])
                        for j in range(HC):
                            mm = pe.transpose(ffn_ps[3][:, j * NB:(j + 1) * NB], bias_in[:, j * P:(j + 1) * P],
                                              ident[0:NB, 0:NB])
                        mm.then_inc(s_wT, 1)
                    for m in weights_of(s, n):
                        l, e = matrix(m)
                        pe.wait_ge(s_wload[m % NIN], 16 * (m // NIN + 1))
                        if m >= 2:
                            pe.wait_ge(s_wfold, m - 1)
                        for kc in range(HC):
                            for hc in range(HC):
                                mm = pe.transpose(ffn_ps[m % 2][:, (kc * HC + hc) * P:(kc * HC + hc + 1) * P],
                                                  w_in[m % NIN][:, hc, kc * P:(kc + 1) * P], ident[:, :])
                        mm.then_inc(s_wT, 1)
                    if ffn:
                        if n == 0:
                            pe.wait_ge(s_xnf, k + 1)
                            if isinstance(s, int) and s == 2:
                                pe.wait_ge(s_bias, 1)
                                pe.wait_ge(s_wfold, NW)
                            else:
                                pe.wait_ge(s_y, 2 * k)
                            for i in range(IT):
                                mm = pe.transpose(ffn_ps[i // 4][:, (i % 4) * P:(i % 4 + 1) * P], xnf[:, i, :],
                                                  ident[:, :])
                                if i % 4 == 3:
                                    mm.then_inc(s_nT, 1)
                            pe.wait_ge(s_hub, HUBS * (k + 1))
                            for h in range(HUBS):
                                mm = pe.transpose(ffn_ps[2][:, h * P:(h + 1) * P], hub[:, h, :], ident[:, :])
                            mm.then_inc(s_nT, 1)
                        if n == 1:
                            pe.wait_ge(s_nTc, 3 * k + 3)
                            pe.wait_ge(s_agg, CHUNKS * (k + 1))
                            for i in range(IT):
                                if i % 4 == 0:
                                    start_with_bias(ffn_ps[i // 4][:, :], 0)
                                o = ffn_ps[i // 4][:, (i % 4) * P:(i % 4 + 1) * P]
                                a = hubT[:, i, :] if i < HUBS else aggT[:, (i - HUBS) * P:(i - HUBS + 1) * P]
                                pe.matmul(o, xnT[:, i, :], gw[:, 0, :], start=False, stop=False)
                                mm = pe.matmul(o, a, gw[:, 1, :], start=False, stop=(i % 4 == 3))
                                if i % 4 == 3:
                                    mm.then_inc(s_gnn, 1)
                        if n in IN_AT:
                            g = IN_AT.index(n)
                            pe.wait_ge(s_h0c, 2 * k + 1 + g)
                            for j in range(HC):
                                mm = pe.matmul(ffn_ps[2 * (1 - g) + j][:, :], wiT[:, j * P:(j + 1) * P],
                                               h0T[:, 4 * g:4 * g + 4, :].rearrange("p t c -> p (t c)"),
                                               start=True, stop=True)
                            mm.then_inc(s_in, 1)
                        for l in range(L):
                            if l == 0 and n in LAYER_AT[0]:
                                pe.wait_ge(s_inr, 2 * k + 2)
                            for i in LAYER_AT[l].get(n, []):
                                pe.wait_ge(s_w[i], (k * L + l + 1) * 16)
                                if l == 1 and i == 0:
                                    pe.wait_ge(s_r[0], (k + 1) * IT)
                                if i >= 4:
                                    pe.wait_ge(s_r[l], k * IT + i - 3)
                                for j in range(HC):
                                    c1 = (i // 4) * HID + j * P
                                    for kc in range(HC):
                                        c0 = kc * HID + j * P
                                        mm = pe.matmul(ffn_ps[i % 4][:, c1:c1 + P], wst[:, i, c0:c0 + P],
                                                       hT[:, l, kc, i, :], start=(kc == 0), stop=(kc == HC - 1))
                                mm.then_inc(s_l[l], 1)
                        if n == OUT_AT:
                            pe.wait_ge(s_r[1], (k + 1) * IT)
                            for i in range(IT):
                                o = ffn_ps[i // 4][:, (i % 4) * P:(i % 4 + 1) * P]
                                if i % 4 == 0:
                                    start_with_bias(ffn_ps[i // 4][:, :], 1)
                                for kc in range(HC):
                                    mm = pe.matmul(o, hT[:, 0, kc, i, :], woT[:, kc, :], start=False,
                                                   stop=(i % 4 == 3 and kc == HC - 1))
                                if i % 4 == 3:
                                    mm.then_inc(s_o, 1)
                    if prep:
                        if n == TT:
                            pe.wait_ge(s_at, (s + 1) * TT)
                            for c in range(CHUNKS):
                                for jt in range(IT):
                                    mm = pe.matmul(prep_f[c][0:NG + 1, 0:CW], pick[:, jt, :],
                                                   at[:, jt, c * CW:(c + 1) * CW], start=(jt == 0),
                                                   stop=(jt == IT - 1))
                            mm.then_inc(s_cnt, 1)
                        rank_tiles(s, RANK_BEFORE.get(n, []))
                    if slots:
                        c, g = n // NG, n % NG
                        K = pe.value_load(pairs[g:g + 1, 1 - even, c:c + 1], min_val=2, max_val=(TOPK + 1) // 2)
                        with pe.Fori(1, K):
                            for bank in range(2):
                                slot(1 - even, *GROUPS[g], bank)
                        if n + 1 < POS:
                            for bank in range(2):
                                slot(1 - even, *GROUPS[(n + 1) % NG], bank)
                    if prep:
                        if n < TT:
                            pe.wait_ge(s_mask, s * TT + n + 1)
                            if n >= 2:
                                pe.wait_ge(s_at, s * TT + n - 1)
                            elif not (isinstance(s, int) and s == 0):
                                pe.wait_ge(s_q, 2 * IT * s)
                            for jt in range(IT):
                                mm = pe.transpose(prep_ps[n % 2][:, jt * P:(jt + 1) * P],
                                                  mask[:, n % 2, jt * P:(jt + 1) * P], identb[:, :])
                            mm.then_inc(s_tr, 1)
                        rank_tiles(s, RANK_AFTER.get(n, []))
                    if ffn and n == 3:
                        pe.wait_ge(s_h0, k + 1)
                        for i in range(IT):
                            mm = pe.transpose(ffn_ps[i // 4][:, (i % 4) * P:(i % 4 + 1) * P], h0[:, i, :],
                                              ident[:, :])
                            if i % 4 == 3:
                                mm.then_inc(s_h0T, 1)
            rounds(pe, round_)

            def tile_again(t, b, one, dma):
                pe.wait_ge(s_const, CONSTS)
                pe.wait_ge(r_xn, one)
                pe.transpose(ffn_ps[0][:, 0:P], xnf[:, 0, :], ident[:, :])
                pe.wait_ge(s_const, CONSTS)
                pe.wait_ge(r_hub, one)
                pe.transpose(ffn_ps[1][:, 0:P], hub[:, 0, :], ident[:, :]).then_inc(r_T, 1)
                pe.wait_ge(s_const, CONSTS)
                pe.wait_ge(r_Tc, one)
                start_with_bias(ffn_ps[0][:, :], 0)
                pe.matmul(ffn_ps[0][:, 0:C], xnT[:, 0, :], gw[:, 0, :], start=False, stop=False)
                pe.matmul(ffn_ps[0][:, 0:C], hubT[:, 0, :], gw[:, 1, :], start=False, stop=True).then_inc(r_gnn, 1)
                pe.wait_ge(s_const, CONSTS)
                pe.wait_ge(r_h0, one)
                pe.transpose(ffn_ps[1][:, 0:P], h0[:, 0, :], ident[:, :]).then_inc(r_h0T, 1)
                pe.wait_ge(s_const, CONSTS)
                pe.wait_ge(r_h0c, one)
                for j in range(HC):
                    mm = pe.matmul(ffn_ps[2][:, j * P:(j + 1) * P], wiT[:, j * P:(j + 1) * P], h0T[:, 0, :],
                                   start=True, stop=True)
                mm.then_inc(r_in, 1)
                for l in range(L):
                    pe.wait_ge(s_const, CONSTS)
                    pe.wait_ge(r_w[l], dma)
                    pe.wait_ge(r_r[l - 1] if l else r_inr, one)
                    for j in range(HC):
                        for kc in range(HC):
                            c0 = kc * HID + j * P
                            mm = pe.matmul(ffn_ps[l][:, j * P:(j + 1) * P], wst[:, l, c0:c0 + P],
                                           hT[:, l, kc, 0, :], start=(kc == 0), stop=(kc == HC - 1))
                    mm.then_inc(r_l[l], 1)
                pe.wait_ge(s_const, CONSTS)
                pe.wait_ge(r_r[L - 1], one)
                start_with_bias(ffn_ps[3][:, :], 1)
                for kc in range(HC):
                    mm = pe.matmul(ffn_ps[3][:, 0:C], hT[:, 0, kc, 0, :], woT[:, kc, :], start=False,
                                   stop=(kc == HC - 1))
                mm.then_inc(r_o, 1)
            again(pe, tile_again)

        @block.vector
        def _(dve):
            def step(ins):
                dve.drain()

            slots_seen = dve.alloc_register("slots_seen")
            dve.reg_mov(slots_seen, 0)
            chunks_clear = dve.alloc_register("chunks_clear")
            dve.reg_mov(chunks_clear, 0)
            dve.wait_ge(s_const, CONSTS)
            dve.memset(newton[:, 0, :], 0.0).then_inc(s_max, 1)
            dve.memset(newton[:, 1, :], 0.0).then_inc(s_max, 1)

            def newton_rstd(out_r, v, sd, tmp):
                r, e = tmp[:, 0, :], tmp[:, 1, :]
                step(dve.reciprocal(r, sd))
                step(dve.tensor_tensor(e, r, r, ALU.mult))
                step(dve.tensor_tensor(e, e, v, ALU.mult))
                step(dve.tensor_scalar(e, e, -0.5, 1.5, ALU.mult, ALU.add))
                step(dve.tensor_tensor(out_r, r, e, ALU.mult))

            def one_hot(par, first, many, c, bank, r):
                dve.tensor_scalar(onehot[:, bank, 0:many, :], rank[:, par, first:first + many, c * CW:(c + 1) * CW],
                                  r, None, ALU.is_equal).then_inc(s_onehot, 1)

            def fold_slot(c, bank):
                dve.tensor_tensor(acc[:, c, bank, :], slot_ps[bank][:, 0:CW], acc[:, c, bank, :],
                                  ALU.max).then_inc(s_max, 1)

            def next_slot():
                dve.reg_add(slots_seen, slots_seen, 1)
                dve.wait_ge(s_slot, slots_seen)

            def round_(s, even, prep, slots, ffn):
                k = s - 2
                for n in range(POS):
                    c, g = n // NG, n % NG
                    par = 1 - even
                    if slots and n == 0:
                        dve.wait_ge(s_q, 2 * IT * (s - 1) + 2)
                        for bank in range(2):
                            one_hot(par, *GROUPS[0], 0, bank, ranks[:, bank:bank + 1])
                    if prep:
                        prepare(s, even, n)
                    for m in weights_of(s, n):
                        fold_weights(m)
                    if slots:
                        first, many = GROUPS[g]
                        if g == 0:
                            dve.reg_add(chunks_clear, chunks_clear, 1)
                            dve.wait_ge(s_const, CONSTS)
                            dve.wait_ge(s_clear, chunks_clear)
                        if n == 0:
                            dve.wait_ge(s_pairs, s)
                        K = dve.value_load(pairs[g:g + 1, par, c:c + 1], min_val=2, max_val=(TOPK + 1) // 2)
                        with dve.Fori(1, K) as j:
                            for bank in range(2):
                                next_slot()
                                one_hot(par, first, many, c, bank, ranks[:, bass.ds(j * 2 + bank, 1)])
                                fold_slot(c, bank)
                        if n + 1 < NG:
                            dve.wait_ge(s_q, 2 * IT * (s - 1) + 2 * sum(GROUPS[g + 1]))
                        for bank in range(2):
                            next_slot()
                            if n + 1 < POS:
                                one_hot(par, *GROUPS[(n + 1) % NG], (n + 1) // NG, bank, ranks[:, bank:bank + 1])
                            fold_slot(c, bank)
                        if g == NG - 1:
                            dve.drain()
                            if ffn and c == 0:
                                dve.wait_ge(s_gnn, 2 * (s - 1))
                            dve.tensor_tensor(aggT[:, c * CW:(c + 1) * CW], acc[:, c, 0, :], acc[:, c, 1, :],
                                              ALU.max).then_inc(s_agg, 1)
                        if n in REDUCE_AT:
                            reduce_hub(s, REDUCE_AT.index(n), ffn)
                    if ffn:
                        finish(s, k, n)

            def prepare(s, even, n):
                own = some(s * IT, IT)
                if n == 0:
                    if isinstance(s, int):
                        if s in (0, 1, 2, 4):
                            dve.wait_ge(s_x[min(s, 3)], 16 * (1, 1, 2, 0, B - 4)[s])
                    else:
                        dve.wait_ge(s_x[3], 16 * (B - 4))
                    for i in range(IT):
                        dve.bn_stats(stats[:, i, :], xs[:, some(s * IT + i), :].rearrange("p a c -> p (a c)"))
                    dve.drain()
                    for i in range(IT):
                        dve.bn_aggr(mv[:, i, :], stats[:, i, :])
                    dve.drain()
                    dve.tensor_scalar(mv[:, :, 1], mv[:, :, 1], EPS, None, ALU.add).then_inc(s_var1, 1)
                if n == 1:
                    dve.wait_ge(s_std1, s + 1)
                    newton_rstd(rstd1[:, own], mv[:, :, 1], std[:, :], newton)
                    dve.scalar_tensor_tensor(out=shift1[:, own], in0=mv[:, :, 0], scalar=-1.0, in1=rstd1[:, own],
                                             op0=ALU.mult, op1=ALU.mult).then_inc(s_norm1, 1)
                if n == 7:
                    dve.wait_ge(s_cnt, s + 1)
                    for c in range(CHUNKS):
                        dve.tensor_reduce(most[:, some(s * TT + c * TT // CHUNKS, TT // CHUNKS)],
                                          prep_f[c][0:NG + 1, 0:CW].rearrange("p (t i) -> p t i", i=P),
                                          AX_X, ALU.max)
                    dve.drain()
                    step(dve.tensor_reduce(mostc[:, 0, :],
                                           most[:, some(s * TT, TT)].rearrange("p (c t) -> p c t", c=CHUNKS),
                                           AX_X, ALU.max))
                    step(dve.tensor_scalar(mostc[:, 1, :], mostc[:, 0, :], 0.5, 0.25, ALU.mult, ALU.add))
                    step(dve.tensor_scalar(mostc[:, 1, :], mostc[:, 1, :], ROUNDER, ROUNDER, ALU.add, ALU.subtract))
                    dve.tensor_scalar(pairs[:, even, :], mostc[:, 1, :], 2.0, float((TOPK + 1) // 2), ALU.max,
                                      ALU.min).then_inc(s_pairs, 1)
                if n == SCORE_AT:
                    for h in range(HUBS):
                        q = ORDER.index(h)
                        dve.wait_ge(s_adj[q % 4], 32 * s + 16 * (q // 4 + 1))
                        dve.scalar_tensor_tensor(out=score[:, h, :], in0=adj_sb[:, q % 4, :], scalar=0.0,
                                                 in1=down[:, :], op0=ALU.not_equal,
                                                 op1=ALU.mult).then_inc(s_scored, 1)
                if n in TOP_AT:
                    r = TOP_AT.index(n)
                    dve.drain()
                    for h in range(HUBS):
                        dve.max(top[:, h, 8 * r:8 * r + 8], score[:, h, :])
                    dve.drain()
                    if r < ROUNDS - 1:
                        for h in range(HUBS):
                            dve.match_replace(score[:, h, :], top[:, h, 8 * r:8 * r + 8], score[:, h, :], 0.0)
                    else:
                        dve.tensor_scalar(floor[:, :], top[:, :, TOPK], 0.0, NEG_BIG, ALU.is_gt, ALU.mult)
                        dve.tensor_scalar(idx[:, :, :], top[:, :, 0:TOPK], -1.0, base[:, some(s)],
                                          ALU.mult, ALU.add).then_inc(s_idx, HUBS)

            def reduce_hub(s, h, ffn):
                b = s - 1
                dve.wait_ge(s_gath, (b * HUBS + h + 1) * (16 * TOPK))
                dve.tensor_reduce(hub_max[:, :], gath[:, :, :].rearrange("p k c -> p c k"), AX_X,
                                  ALU.max).then_inc(s_hubred, 1)
                dve.drain()
                if ffn and h == 0:
                    dve.wait_ge(s_nT, 3 * (s - 1))
                dve.tensor_scalar(hub[:, h, :], hub_max[:, :], floor[:, h:h + 1], None, ALU.max).then_inc(s_hub, 1)

            def split_biases():
                part = [bias_rows[:, :, p, :] for p in range(2)]
                row = [ident[0:SPLITS, p:p + 1] for p in range(SPLITS)]
                dve.wait_ge(s_small, SMALL * 16)
                step(dve.tensor_copy(part[0], bias_raw))
                step(dve.tensor_tensor(bias_rest, bias_raw, part[0], ALU.subtract))
                step(dve.tensor_copy(part[1], bias_rest))
                step(dve.tensor_tensor(bias_last, bias_rest, part[1], ALU.subtract))
                step(dve.tensor_scalar(bias_sum, part[0], row[0], None, ALU.mult))
                step(dve.scalar_tensor_tensor(out=bias_sum, in0=part[1], scalar=row[1], in1=bias_sum, op0=ALU.mult,
                                              op1=ALU.add))
                step(dve.scalar_tensor_tensor(out=bias_sum, in0=bias_last, scalar=row[2], in1=bias_sum,
                                              op0=ALU.mult, op1=ALU.add))
                for t in range(BANK // C):
                    ins = dve.tensor_copy(bias_rows[:, :, t, :], bias_sum)
                ins.then_inc(s_bias, 1)
                dve.drain()

            def fold_weights(m):
                l, e = matrix(m)
                if m == 0:
                    dve.wait_ge(s_wT, 1)
                    dve.tensor_copy(wiT[:, :], ffn_ps[2][:, 0:HID])
                    dve.tensor_copy(woT[:, :, :].rearrange("p j n -> p (j n)"), ffn_ps[2][:, HID:HID + HC * C])
                    step(dve.tensor_copy(biasT[:, :, :].rearrange("p j n -> p (j n)"), ffn_ps[3][:, 0:HC * NB]))
                    for ll in range(L):
                        for j in range(HC):
                            shared = biasT[:, j, L * NE + ll:L * NE + ll + 1]
                            dve.tensor_scalar(bias[:, 0:NE, ll, j], biasT[:, j, ll * NE:(ll + 1) * NE], shared, None,
                                              ALU.add)
                            dve.tensor_copy(bias[:, NE, ll, j:j + 1], shared)
                    dve.drain()
                    split_biases()
                    dve.wait_ge(s_small, SMALL * 16)
                    rf, ok = route_f[:, 0, :], route_f[:, 1, :]
                    step(dve.tensor_copy(rf, route_in[:, :]))
                    step(dve.tensor_scalar(ok, rf, 0.0, None, ALU.is_ge))
                    step(dve.scalar_tensor_tensor(out=ok, in0=rf, scalar=float(NE), in1=ok, op0=ALU.is_lt,
                                                  op1=ALU.mult))
                    step(dve.scalar_tensor_tensor(out=rf, in0=rf, scalar=float(NE), in1=ok, op0=ALU.subtract,
                                                  op1=ALU.mult))
                    dve.tensor_scalar(route[:, :], rf, float(NE), None, ALU.add).then_inc(s_route, 1)
                dve.wait_ge(s_wT, m + 2)
                if m >= NST:
                    dve.wait_ge(s_wstore[m % NST], 16 * (m // NST))
                o = wst[:, m % NST, 0:HC * HID]
                dve.tensor_copy(wst[:, m % NST, HC * HID:WROW], bias[:, e, l, :])
                if m < L:
                    step(dve.tensor_copy(wsI[:, l, :], ffn_ps[m % 2][:, :]))
                    for j in range(HC):
                        c0 = j * HID + j * P
                        dve.tensor_tensor(wsI[:, l, c0:c0 + P], wsI[:, l, c0:c0 + P], ident[:, :], ALU.add)
                    dve.drain()
                    dve.tensor_copy(o, wsI[:, l, :]).then_inc(s_wfold, 1)
                else:
                    dve.tensor_tensor(o, ffn_ps[m % 2][:, :], wsI[:, l, :], ALU.add).then_inc(s_wfold, 1)

            def finish(s, k, n):
                if n == 1:
                    for g in range(2):
                        dve.wait_ge(s_gnn, 2 * k + g + 1)
                        t = some(k * IT + 4 * g, 4)
                        dve.scalar_tensor_tensor(out=x1[:, 4 * g:4 * g + 4, :].rearrange("p t c -> p (t c)"),
                                                 in0=ffn_ps[g][:, :], scalar=0.0,
                                                 in1=xs[:, t, :].rearrange("p t c -> p (t c)"), op0=ALU.max,
                                                 op1=ALU.add)
                    dve.drain()
                    for i in range(IT):
                        dve.bn_stats(st2[:, i, :], x1[:, i, :])
                    dve.drain()
                    for i in range(IT):
                        dve.bn_aggr(mv2[:, i, :], st2[:, i, :])
                    dve.drain()
                    dve.tensor_scalar(mv2[:, :, 1], mv2[:, :, 1], EPS, None, ALU.add).then_inc(s_var2, 1)
                if n == 2:
                    dve.wait_ge(s_std2, k + 1)
                    newton_rstd(r2[:, :], mv2[:, :, 1], std2[:, :], newton)
                    dve.scalar_tensor_tensor(out=shift2[:, :], in0=mv2[:, :, 0], scalar=-1.0, in1=r2[:, :],
                                             op0=ALU.mult, op1=ALU.mult).then_inc(s_norm2, 1)
                if n == OUT_AT:
                    for g in range(2):
                        dve.wait_ge(s_o, 2 * k + g + 1)
                        dve.tensor_tensor(y[:, 4 * g:4 * g + 4, :].rearrange("p t c -> p (t c)"), ffn_ps[g][:, :],
                                          x1[:, 4 * g:4 * g + 4, :].rearrange("p t c -> p (t c)"),
                                          ALU.add).then_inc(s_y, 1)
            rounds(dve, round_)

            step(dve.tensor_reduce(most_any[:, :], most[:, :], AX_X, ALU.max))
            dve.tensor_scalar(over[:, :], most[:, :], float(TOPK), None, ALU.is_gt)
            dve.tensor_scalar(over_any[:, :], most_any[:, :], float(TOPK), None, ALU.is_gt).then_inc(s_over, 1)

            gathered = dve.alloc_register("gathered")
            dve.reg_mov(gathered, 0)

            def tile_again(t, b, one, dma):
                one_tile = bass.ds(t, 1)
                dve.reg_add(gathered, gathered, 16 * TOPK)
                dve.wait_ge(s_const, CONSTS)
                dve.wait_ge(r_adj, dma)
                step(dve.scalar_tensor_tensor(out=score[:, 0, :], in0=adj_sb[:, 0, :], scalar=0.0, in1=down[:, :],
                                              op0=ALU.not_equal, op1=ALU.mult))
                for r in range(ROUNDS):
                    step(dve.max(top[:, 0, 8 * r:8 * r + 8], score[:, 0, :]))
                    if r < ROUNDS - 1:
                        step(dve.match_replace(score[:, 0, :], top[:, 0, 8 * r:8 * r + 8], score[:, 0, :], 0.0))
                dve.tensor_scalar(floor[:, 0:1], top[:, 0, TOPK:TOPK + 1], 0.0, NEG_BIG, ALU.is_gt, ALU.mult)
                step(dve.tensor_scalar(idx[:, 0, :], top[:, 0, 0:TOPK], -1.0, base[:, bass.ds(b, 1)],
                                       ALU.mult, ALU.add).then_inc(r_idx, 1))
                dve.wait_ge(s_const, CONSTS)
                dve.wait_ge(r_gath, gathered)
                step(dve.tensor_reduce(hub_max[:, :], gath[:, :, :].rearrange("p k c -> p c k"), AX_X, ALU.max))
                step(dve.tensor_scalar(hub[:, 0, :], hub_max[:, :], floor[:, 0:1], None, ALU.max).then_inc(r_hub, 1))
                dve.wait_ge(s_const, CONSTS)
                dve.wait_ge(r_gnn, one)
                step(dve.scalar_tensor_tensor(out=x1[:, 0, :], in0=ffn_ps[0][:, 0:C], scalar=0.0,
                                              in1=xs[:, one_tile, :].rearrange("p t c -> p (t c)"), op0=ALU.max,
                                              op1=ALU.add))
                step(dve.bn_stats(st2[:, 0, :], x1[:, 0, :]))
                step(dve.bn_aggr(mv2[:, 0, :], st2[:, 0, :]))
                step(dve.tensor_scalar(mv2[:, 0, 1:2], mv2[:, 0, 1:2], EPS, None, ALU.add).then_inc(r_var, 1))
                dve.wait_ge(s_const, CONSTS)
                dve.wait_ge(r_std, one)
                newton_rstd(r2[:, 0:1], mv2[:, 0, 1:2], std2[:, 0:1], newton[:, :, 0:1])
                step(dve.tensor_scalar(h0[:, 0, :], x1[:, 0, :], mv2[:, 0, 0:1], r2[:, 0:1], ALU.subtract,
                                       ALU.mult).then_inc(r_h0, 1))
                dve.wait_ge(s_const, CONSTS)
                dve.wait_ge(r_o, one)
                step(dve.tensor_tensor(y[:, 0, :], ffn_ps[3][:, 0:C], x1[:, 0, :], ALU.add).then_inc(r_y, 1))
            again(dve, tile_again)


_INS = ['x', 'adj', 'L0_gnn_W', 'L0_gnn_b', 'L0_ffn_route_id', 'L0_ffn_Wi', 'L0_ffn_bi', 'L0_ffn_Wr', 'L0_ffn_br',
        'L0_ffn_Ws', 'L0_ffn_bs', 'L0_ffn_Wo', 'L0_ffn_bo']
_OUTS = [((8, 1024, 128), 'float32')]


def kernel(**inputs):
    import numpy as _np
    import concourse.bacc as _bacc
    from concourse import mybir as _mybir
    from concourse.bass_utils import run_bass_kernel_spmd as _run

    nc = _bacc.Bacc("TRN2", target_bir_lowering=False, num_devices=1)
    arrays, args = {}, []
    for name in _INS:
        a = _np.ascontiguousarray(inputs[name])
        arrays[f"in_{name}_dram"] = a
        args.append(nc.dram_tensor(f"in_{name}_dram", a.shape, _mybir.dt.from_np(a.dtype), kind="ExternalInput").ap())
    for i, (shape, dtype) in enumerate(_OUTS):
        dt = _mybir.dt.from_np(_np.dtype(dtype))
        args.append(nc.dram_tensor(f"out_{i}_dram", shape, dt, kind="ExternalOutput").ap())
    gnn_ffn_program(nc, *args)
    r = _run(nc, [arrays], core_ids=[0])
    got = tuple(r.results[0][f"out_{i}_dram"] for i in range(len(_OUTS)))
    return got[0]
```
